# Optimizing a Trainium2 kernel written in Bass

```python
import numpy as np
import jax
import jax.numpy as jnp

def _softmax(x, axis=-1):
    return jax.nn.softmax(x, axis=axis)

def _gelu(x):
    return jax.nn.gelu(x, approximate=True)

def _silu(x):
    return jax.nn.silu(x)

def _sigmoid(x):
    return jax.nn.sigmoid(x)

def _layernorm(x, axis=-1, eps=1e-05):
    m = jnp.mean(x, axis=axis, keepdims=True)
    v = jnp.var(x, axis=axis, keepdims=True)
    return (x - m) / jnp.sqrt(v + eps)

def _scatter_add(tgt, idx, src, axis=0):
    return tgt.at[idx].add(src)

def _segment_sum(src, seg, n):
    return jax.ops.segment_sum(src, seg, n)
kernel_name = 'mk_lm_tower_d1_tok_ids1024_r4_3bb9a3'

def setup_inputs(seed: int=0):
    np.random.seed(seed)
    _w = jnp.asarray

    def _rec_inputs():
        import jax
        import jax.numpy as jnp
        _rk = jax.random.key(seed)
        x = jax.random.randint(jax.random.fold_in(_rk, 1), (8, 256), 0, 29991, jnp.int32)
        return x
    x = _rec_inputs()

    def _L0_tok_setup():
        import jax, jax.numpy as jnp
        import numpy as np
        import math
        B, S, D, H, L, F, V = (8, 125, 256, 16, 4, 1024, 7500)
        DK = D // H
        EPS = 1e-06

        def _layer_norm(x, a, b):
            mean = jnp.mean(x, axis=-1, keepdims=True)
            var = jnp.sum((x - mean) ** 2, axis=-1, keepdims=True) / (x.shape[-1] - 1)
            return a * (x - mean) / (jnp.sqrt(var) + EPS) + b

        def _pos_encoding(seq_len, d_model):
            pos = np.arange(seq_len, dtype=np.float32)[:, None]
            div = np.exp(np.arange(0, d_model, 2, dtype=np.float32) * -(math.log(10000.0) / d_model))
            pe = np.zeros((seq_len, d_model), dtype=np.float32)
            pe[:, 0::2] = np.sin(pos * div)
            pe[:, 1::2] = np.cos(pos * div)
            return jnp.asarray(pe)
        key = jax.random.key(seed)
        ks = jax.random.split(key, 12)
        s = 0.02
        return {'x': jax.random.randint(ks[0], (B, S), 0, V), 'emb': jax.random.normal(ks[1], (V, D), jnp.float32) * s, 'attn_w': jax.random.normal(ks[2], (L, 4, D, D), jnp.float32) * s, 'attn_b': jnp.zeros((L, 4, D), jnp.float32), 'ln_a': jnp.ones((L, 2, D), jnp.float32), 'ln_b': jnp.zeros((L, 2, D), jnp.float32), 'w1': jax.random.normal(ks[3], (L, D, F), jnp.float32) * s, 'b1': jnp.zeros((L, F), jnp.float32), 'w2': jax.random.normal(ks[4], (L, F, D), jnp.float32) * s, 'b2': jnp.zeros((L, D), jnp.float32), 'norm_a': jnp.ones((D,), jnp.float32), 'norm_b': jnp.zeros((D,), jnp.float32)}
    _L0_tok_all = _L0_tok_setup()
    _L0_tok_in = {k: v for k, v in _L0_tok_all.items() if k in ('emb', 'attn_w', 'attn_b', 'ln_a', 'ln_b', 'w1', 'b1', 'w2', 'b2', 'norm_a', 'norm_b')}
    del _L0_tok_all

    def _L0_attn_setup():
        import jax, jax.numpy as jnp
        import numpy as np
        HEADS = 16
        DIM_HEAD = 64
        SEG = 128
        P = 16

        def rmsnorm(x, g, eps=1e-06):
            var = jnp.mean(x * x, axis=-1, keepdims=True)
            return x * jax.lax.rsqrt(var + eps) * g
        key = jax.random.key(seed)
        ks = jax.random.split(key, 6)
        B, S, D = (2, 1024, 256)
        inner = HEADS * DIM_HEAD
        return {'x': jax.random.normal(ks[0], (B, S, D), jnp.float32), 'gamma': jnp.ones((D,), jnp.float32), 'w_qkv': jax.random.normal(ks[1], (D, inner * 3), jnp.float32) * D ** (-0.5), 'w_out': jax.random.normal(ks[2], (inner, D), jnp.float32) * inner ** (-0.5), 'pm_k': jax.random.normal(ks[3], (HEADS, P, DIM_HEAD), jnp.float32) * 0.02, 'pm_v': jax.random.normal(ks[4], (HEADS, P, DIM_HEAD), jnp.float32) * 0.02}
    _L0_attn_all = _L0_attn_setup()
    _L0_attn_in = {k: v for k, v in _L0_attn_all.items() if k in ('gamma', 'w_qkv', 'w_out', 'pm_k', 'pm_v')}
    del _L0_attn_all

    def _L0_ffn_setup():
        import math
        import jax, jax.numpy as jnp
        import numpy as np
        B, T, D, H, E, K, S = (4, 1024, 256, 512, 16, 2, 2)
        ROUTE_SCALE = 1.0

        def _swiglu(x, w1, w3, w2):
            return jax.nn.silu(x @ w1) * (x @ w3) @ w2
        key = jax.random.key(seed)
        ks = jax.random.split(key, 9)
        s = 0.02
        return {'x': jax.random.normal(ks[0], (B, T, D), jnp.float32), 'gate_w': jax.random.normal(ks[1], (D, E), jnp.float32) * s, 'gate_b': jnp.zeros((E,), jnp.float32), 'ew1': jax.random.normal(ks[2], (E, D, H), jnp.float32) * s, 'ew3': jax.random.normal(ks[3], (E, D, H), jnp.float32) * s, 'ew2': jax.random.normal(ks[4], (E, H, D), jnp.float32) * s, 'sw1': jax.random.normal(ks[5], (S, D, H), jnp.float32) * s, 'sw3': jax.random.normal(ks[6], (S, D, H), jnp.float32) * s, 'sw2': jax.random.normal(ks[7], (S, H, D), jnp.float32) * s}
    _L0_ffn_all = _L0_ffn_setup()
    _L0_ffn_in = {k: v for k, v in _L0_ffn_all.items() if k in ('gate_w', 'gate_b', 'ew1', 'ew3', 'ew2', 'sw1', 'sw3', 'sw2')}
    del _L0_ffn_all
    return {'x': x, 'L0_tok_emb': _L0_tok_in['emb'], 'L0_tok_attn_w': _L0_tok_in['attn_w'], 'L0_tok_attn_b': _L0_tok_in['attn_b'], 'L0_tok_ln_a': _L0_tok_in['ln_a'], 'L0_tok_ln_b': _L0_tok_in['ln_b'], 'L0_tok_w1': _L0_tok_in['w1'], 'L0_tok_b1': _L0_tok_in['b1'], 'L0_tok_w2': _L0_tok_in['w2'], 'L0_tok_b2': _L0_tok_in['b2'], 'L0_tok_norm_a': _L0_tok_in['norm_a'], 'L0_tok_norm_b': _L0_tok_in['norm_b'], 'L0_attn_gamma': _L0_attn_in['gamma'], 'L0_attn_w_qkv': _L0_attn_in['w_qkv'], 'L0_attn_w_out': _L0_attn_in['w_out'], 'L0_attn_pm_k': _L0_attn_in['pm_k'], 'L0_attn_pm_v': _L0_attn_in['pm_v'], 'L0_ffn_gate_w': _L0_ffn_in['gate_w'], 'L0_ffn_gate_b': _L0_ffn_in['gate_b'], 'L0_ffn_ew1': _L0_ffn_in['ew1'], 'L0_ffn_ew3': _L0_ffn_in['ew3'], 'L0_ffn_ew2': _L0_ffn_in['ew2'], 'L0_ffn_sw1': _L0_ffn_in['sw1'], 'L0_ffn_sw3': _L0_ffn_in['sw3'], 'L0_ffn_sw2': _L0_ffn_in['sw2']}

def reference(x, L0_tok_emb, L0_tok_attn_w, L0_tok_attn_b, L0_tok_ln_a, L0_tok_ln_b, L0_tok_w1, L0_tok_b1, L0_tok_w2, L0_tok_b2, L0_tok_norm_a, L0_tok_norm_b, L0_attn_gamma, L0_attn_w_qkv, L0_attn_w_out, L0_attn_pm_k, L0_attn_pm_v, L0_ffn_gate_w, L0_ffn_gate_b, L0_ffn_ew1, L0_ffn_ew3, L0_ffn_ew2, L0_ffn_sw1, L0_ffn_sw3, L0_ffn_sw2):
    import jax
    import jax.numpy as jnp

    def _L0_tok_ref(x, emb, attn_w, attn_b, ln_a, ln_b, w1, b1, w2, b2, norm_a, norm_b):
        import jax, jax.numpy as jnp
        import numpy as np
        import math
        B, S, D, H, L, F, V = (8, 125, 256, 16, 4, 1024, 7500)
        DK = D // H
        EPS = 1e-06

        def _layer_norm(x, a, b):
            mean = jnp.mean(x, axis=-1, keepdims=True)
            var = jnp.sum((x - mean) ** 2, axis=-1, keepdims=True) / (x.shape[-1] - 1)
            return a * (x - mean) / (jnp.sqrt(var) + EPS) + b

        def _pos_encoding(seq_len, d_model):
            pos = np.arange(seq_len, dtype=np.float32)[:, None]
            div = np.exp(np.arange(0, d_model, 2, dtype=np.float32) * -(math.log(10000.0) / d_model))
            pe = np.zeros((seq_len, d_model), dtype=np.float32)
            pe[:, 0::2] = np.sin(pos * div)
            pe[:, 1::2] = np.cos(pos * div)
            return jnp.asarray(pe)
        b, s = x.shape
        h = emb[x] + _pos_encoding(s, D)
        inv_sqrt_dk = 1.0 / math.sqrt(DK)
        for l in range(L):
            y = _layer_norm(h, ln_a[l, 0], ln_b[l, 0])
            qkv = jnp.einsum('bsd,tde->tbse', y, attn_w[l, :3]) + attn_b[l, :3][:, None, None, :]
            q, k, v = [t.reshape(b, s, H, DK).transpose(0, 2, 1, 3) for t in qkv]
            scores = jnp.einsum('bhqd,bhkd->bhqk', q, k) * inv_sqrt_dk
            p = jax.nn.softmax(scores, axis=-1)
            o = jnp.einsum('bhqk,bhkd->bhqd', p, v).transpose(0, 2, 1, 3).reshape(b, s, D)
            h = h + o @ attn_w[l, 3] + attn_b[l, 3]
            y = _layer_norm(h, ln_a[l, 1], ln_b[l, 1])
            h = h + jax.nn.relu(y @ w1[l] + b1[l]) @ w2[l] + b2[l]
        return _layer_norm(h, norm_a, norm_b)

    def _L0_attn_ref(x, gamma, w_qkv, w_out, pm_k, pm_v):
        import jax, jax.numpy as jnp
        import numpy as np
        HEADS = 16
        DIM_HEAD = 64
        SEG = 128
        P = 16

        def rmsnorm(x, g, eps=1e-06):
            var = jnp.mean(x * x, axis=-1, keepdims=True)
            return x * jax.lax.rsqrt(var + eps) * g
        B, S, D = x.shape
        pad = -S % SEG
        Sp = S + pad
        nw = Sp // SEG
        h = rmsnorm(x, gamma)
        qkv = h @ w_qkv
        q, k, v = jnp.split(qkv, 3, axis=-1)

        def fold(t):
            t = jnp.pad(t, ((0, 0), (0, pad), (0, 0)))
            t = t.reshape(B, nw, SEG, HEADS, DIM_HEAD)
            return t.transpose(0, 1, 3, 2, 4)
        q, k, v = (fold(q), fold(k), fold(v))
        pmk = jnp.broadcast_to(pm_k, (B, nw, HEADS, P, DIM_HEAD))
        pmv = jnp.broadcast_to(pm_v, (B, nw, HEADS, P, DIM_HEAD))
        k = jnp.concatenate([pmk, k], axis=3)
        v = jnp.concatenate([pmv, v], axis=3)
        scale = DIM_HEAD ** (-0.5)
        sim = jnp.einsum('bwhid,bwhjd->bwhij', q, k) * scale
        qi = jnp.arange(SEG)[:, None]
        kj = jnp.arange(SEG + P)[None, :] - P
        mask = (kj < 0) | (qi >= kj)
        sim = jnp.where(mask, sim, -jnp.inf)
        attn = jax.nn.softmax(sim, axis=-1)
        out = jnp.einsum('bwhij,bwhjd->bwhid', attn, v)
        out = out.transpose(0, 1, 3, 2, 4).reshape(B, Sp, HEADS * DIM_HEAD)
        out = out[:, :S]
        return out @ w_out

    def _L0_ffn_ref(x, gate_w, gate_b, ew1, ew3, ew2, sw1, sw3, sw2):
        import math
        import jax, jax.numpy as jnp
        import numpy as np
        B, T, D, H, E, K, S = (4, 1024, 256, 512, 16, 2, 2)
        ROUTE_SCALE = 1.0

        def _swiglu(x, w1, w3, w2):
            return jax.nn.silu(x @ w1) * (x @ w3) @ w2
        Bx, Tx, Dx = x.shape
        flat = x.reshape(-1, Dx)
        N = flat.shape[0]
        n_experts = gate_w.shape[1]
        logits = flat @ gate_w
        scores = jax.nn.softmax(logits.astype(jnp.float32), -1) + gate_b
        _, topi = jax.lax.top_k(scores, K)
        weights = jnp.take_along_axis(logits, topi, axis=-1) * ROUTE_SCALE
        weights = weights.astype(flat.dtype)
        capacity = math.ceil(N * K / n_experts * 1.25)

        def per_expert(gid, w1, w3, w2):
            match = topi == gid
            assigned = match.any(-1)
            w_tok = jnp.sum(jnp.where(match, weights, 0.0), -1)
            wm = jnp.where(assigned, w_tok, -jnp.inf)
            vals, idx = jax.lax.top_k(wm, capacity)
            valid = assigned[idx]
            xs = flat[idx]
            y = _swiglu(xs, w1, w3, w2) * jnp.where(valid, vals, 0.0)[:, None]
            return (idx, y)
        idxs, ys = jax.vmap(per_expert)(jnp.arange(n_experts), ew1, ew3, ew2)
        out = jnp.zeros_like(flat).at[idxs.reshape(-1)].add(ys.reshape(-1, Dx))
        shared = jax.vmap(lambda w1, w3, w2: _swiglu(flat, w1, w3, w2))(sw1, sw3, sw2)
        out = out + shared.mean(0)
        return out.reshape(Bx, Tx, Dx)
    h = _L0_tok_ref(x, L0_tok_emb, L0_tok_attn_w, L0_tok_attn_b, L0_tok_ln_a, L0_tok_ln_b, L0_tok_w1, L0_tok_b1, L0_tok_w2, L0_tok_b2, L0_tok_norm_a, L0_tok_norm_b)
    h = h + _L0_attn_ref(_layernorm(h, axis=-1), L0_attn_gamma, L0_attn_w_qkv, L0_attn_w_out, L0_attn_pm_k, L0_attn_pm_v)
    h = h + _L0_ffn_ref(_layernorm(h, axis=-1), L0_ffn_gate_w, L0_ffn_gate_b, L0_ffn_ew1, L0_ffn_ew3, L0_ffn_ew2, L0_ffn_sw1, L0_ffn_sw3, L0_ffn_sw2)
    return h

_drawn_inputs = setup_inputs


def setup_inputs(seed=0):
    import zlib

    import numpy as np

    out = dict(_drawn_inputs(seed))
    spreads = {'L0_tok_attn_b': (0.0, 0.1),
     'L0_tok_ln_a': (1.0, 0.2),
     'L0_tok_ln_b': (0.0, 0.1),
     'L0_tok_b1': (0.0, 0.1),
     'L0_tok_b2': (0.0, 0.1),
     'L0_tok_norm_a': (1.0, 0.2),
     'L0_tok_norm_b': (0.0, 0.1),
     'L0_attn_gamma': (1.0, 0.2),
     'L0_ffn_gate_b': (0.0, 0.8)}
    factors = {'L0_attn_pm_k': 8.0,
     'L0_attn_pm_v': 8.0,
     'L0_ffn_gate_w': 8.0,
     'L0_ffn_ew1': 8.0,
     'L0_ffn_ew3': 8.0,
     'L0_ffn_ew2': 8.0,
     'L0_ffn_sw1': 4.096,
     'L0_ffn_sw3': 3.998,
     'L0_ffn_sw2': 3.996}
    for name, (base, spread) in spreads.items():
        noise = np.random.default_rng([zlib.crc32(name.encode()), seed]).standard_normal(out[name].shape)
        drawn = base * np.exp(spread * noise) if base else spread * noise
        out[name] = jnp.asarray(drawn.astype(out[name].dtype))
    for name, factor in factors.items():
        out[name] = (out[name] * factor).astype(out[name].dtype)
    return out
```

```python
import concourse.bass as bass
from concourse import mybir
from contextlib import ExitStack
import numpy as np

F32 = mybir.dt.float32
I32 = mybir.dt.int32
U32 = mybir.dt.uint32
ALU = mybir.AluOpType
ACT = mybir.ActivationFunctionType
AX = mybir.AxisListType

P = 128
B, S, D = 8, 256, 256
NT = S // P
KD = D // P
PAIRS = B // 2
L, H, DK, F, V = 4, 16, 16, 1024, 7500
FT = F // P
TOK_EPS = 1e-6
HEADS2, DH2, PM = 16, 64, 16
INNER = HEADS2 * DH2
CT = INNER // P
KEYS2 = PM + P
LN_EPS, RMS_EPS = 1e-5, 1e-6
E, TOPK, HID, SHARED = 16, 2, 512, 2
N = B * S
CAP = -(-(N * TOPK * 5) // (E * 4))
HT = HID // P
NEG = float(np.finfo(np.float32).min)

C_LNA, C_LNB, C_BQ, C_BK, C_B1, COLS = 0, 4, 8, 10, 12, 20
R_BV, R_BO, R_B2 = 0, 1, 2
BANKS = 4


class Tally:

    def __init__(self, sem, per, credit=0):
        self.sem, self.per, self.credit = sem, per, credit
        self.base, self.n = 0, 0

    def turn(self, t):
        self.base, self.n = t * self.per, 0

    def up(self, ins, by=1):
        ins.then_inc(self.sem, by)
        self.n += by

    def wait(self, eng, n=None, t=None):
        base = self.base if t is None else t * self.per
        eng.wait_ge(self.sem, base + self.credit + (self.n if n is None else n))

    def whole(self):
        assert self.n == self.per, (self.sem, self.n, self.per)


def embed_and_encoder(nc, io, h, wqkv, wout, s_w2):
    ctx = ExitStack()
    with ctx:
        sb = lambda name, shape, dt=F32: ctx.enter_context(nc.sbuf_tensor(name, shape, dt))
        pb = lambda name, shape: ctx.enter_context(nc.psum_tensor(name, shape, F32))
        sem = lambda name: ctx.enter_context(nc.semaphore(name))

        weights = [sb(f"weights{i}", [P, 6144]) for i in range(2)]
        cols = [sb(f"cols{i}", [P, COLS]) for i in range(2)]
        rows = [sb(f"rows{i}", [P, 3, D]) for i in range(2)]
        wqkvo = [w[:, 0:2048].rearrange("p (t k n) -> p t k n", t=4, k=KD) for w in weights]
        w1 = [w[:, 2048:4096].rearrange("p (k n) -> p k n", k=KD) for w in weights]
        w2 = [w[:, 4096:6144].rearrange("p (k n) -> p k n", k=FT) for w in weights]
        ident = sb("ident", [P, P])
        qmask = sb("qmask", [P, 2])
        half = sb("half", [P, NT])
        idx = sb("idx", [P, B * NT], I32)
        idxf = sb("idxf", [P, B * NT])
        idxn = sb("idxn", [P, B * NT])
        idxu = sb("idxu", [P, B * NT], U32)
        pe_sb = sb("pe_sb", [P, NT, D])
        stats = [sb(f"stats{a}", [P, NT, 6]) for a in range(2)]
        mv = [sb(f"mv{a}", [P, NT, 2]) for a in range(2)]
        sd = [sb(f"sd{a}", [P, NT]) for a in range(2)]
        den = [sb(f"den{a}", [P, NT]) for a in range(2)]
        rstd = [sb(f"rstd{a}", [P, NT]) for a in range(2)]
        yn = [sb(f"yn{a}", [P, NT, D]) for a in range(2)]
        yT = [sb(f"yT{a}", [P, KD, S]) for a in range(2)]
        qm = [sb(f"qm{a}", [P, 2, KD, S]) for a in range(2)]
        kT = [sb(f"kT{a}", [P, KD, S]) for a in range(2)]
        v = [sb(f"v{a}", [P, NT, H // 2, 2, 2 * DK]) for a in range(2)]
        nmax = [sb(f"nmax{a}", [P, NT * H]) for a in range(2)]
        rsum = [sb(f"rsum{a}", [P, NT * H]) for a in range(2)]
        rinv = [sb(f"rinv{a}", [P, NT * H]) for a in range(2)]
        probs = [sb(f"probs{i}", [P, 2, S]) for i in range(8)]
        pts = [sb(f"pts{i}", [P, 2, NT, P]) for i in range(4)]
        rb = [sb(f"rb{a}", [P, NT, H, DK]) for a in range(2)]
        rT = [sb(f"rT{a}", [P, KD, S]) for a in range(2)]
        oT = [sb(f"oT{a}", [P, KD, S]) for a in range(2)]
        aT = [sb(f"aT{a}", [P, FT, S]) for a in range(2)]
        scratch = sb("scratch", [P, BANKS + 1])

        bank = [pb(f"bank{i}", [P, 512]) for i in range(BANKS)]
        ptp = [pb(f"ptp{i}", [P, 2, NT, P]) for i in range(2)]
        ops = [pb(f"ops{a}", [P, 512]) for a in range(2)]

        order = ([(a, "yT", 0) for a in (0, 1)] + [(a, n, 0) for a in (0, 1) for n in "qkv"]
                 + [(u // 16, "S", u % 16) for u in range(32)]
                 + [(0, "rT", 0), (0, "wo", 0), (1, "rT", 0), (0, "y2T", 0)] + [(0, "w1", i) for i in range(4)]
                 + [(1, "wo", 0), (0, "w2", 0), (1, "y2T", 0)]
                 + [(1, "w1", i) for i in range(4)] + [(1, "w2", 0)])
        USES = len(order) // BANKS
        assert len(order) % BANKS == 0
        place = {u: (i % BANKS, i // BANKS) for i, u in enumerate(order)}

        s_const = sem("s_const")
        s_idx = sem("s_idx")
        s_gather = sem("s_gather")
        s_h = sem("s_h")
        s_w = [sem(f"s_w{i}") for i in range(2)]
        s_full = [sem(f"s_full{i}") for i in range(BANKS)]
        s_free = [sem(f"s_free{i}") for i in range(BANKS)]
        NLOAD = 3
        FIRST = 4 + 2 + B
        names = dict(yn_ready=4, max_ready=32, pt_full=32, pt_act=16, pt_dve=16, o_full=2,
                     rb_ready=2, oT_ready=2, var_ready=4, sd_ready=4, dve_step=26)
        sems = {n: sem(n) for n in names}

        def tallies():
            return {n: Tally(sems[n], per) for n, per in names.items()}

        def acquire(pe, t, u):
            b, use = place[u]
            pe.wait_ge(s_free[b], t * USES + use + 1)
            return bank[b]

        def filled(ins, u):
            ins.then_inc(s_full[place[u][0]], 1)

        def take(eng, t, u):
            b, use = place[u]
            eng.wait_ge(s_full[b], t * USES + use + 1)
            return bank[b]

        def release(ins, u):
            ins.then_inc(s_free[place[u][0]], 1)

        def evacuated(eng, t, u):
            b, use = place[u]
            eng.wait_ge(s_free[b], t * USES + use + 2)

        def turns(eng):
            with eng.Fori(0, L // 2) as l2:
                for lp in range(2):
                    with eng.Fori(0, PAIRS) as p:
                        yield l2, lp, p, l2 * (2 * PAIRS) + (lp * PAIRS) + p

        block = ctx.enter_context(nc.Block())

        @block.sync
        def _(sp):
            sp.dma_start(idx[:], io["idx"]).then_inc(s_idx, 16)
            sp.dma_start(pe_sb[:], io["pe"]).then_inc(s_const, 16)
            sp.dma_start(ident[:], io["ident"]).then_inc(s_const, 16)
            sp.dma_start(qmask[:], io["qmask"]).then_inc(s_const, 16)
            for l in range(L):
                if l >= 2:
                    sp.wait_ge(sems["dve_step"], FIRST + names["dve_step"] * (l - 1) * PAIRS)
                sp.dma_start(weights[l % 2][:], io["wtok"][l]).then_inc(s_w[l % 2], 16)
                sp.dma_start(cols[l % 2][:], io["cols"][l]).then_inc(s_w[l % 2], 16)
                sp.dma_start(rows[l % 2][:], io["rows"][l].partition_broadcast(P)).then_inc(s_w[l % 2], 16)
            sp.dma_start(wqkv[:], io["wqkv"]).then_inc(s_w2, 16)
            sp.dma_start(wout[:], io["wout"]).then_inc(s_w2, 16)

        @block.gpsimd
        def _(pool):
            nc.gpsimd.memset(half[:], 0.5).then_inc(sems["sd_ready"], 1)
            pool.wait_ge(s_idx, 17)
            for j in range(B * NT):
                pool.indirect_dma_start(h[:, j // NT, j % NT, :], None, io["emb"],
                                        bass.IndirectOffsetOnAxis(ap=idxu[:, j:j + 1], axis=0)).then_inc(s_gather, 16)
            pool.wait_ge(sems["sd_ready"], 1)
            T = tallies()
            for l2, lp, p, t in turns(pool):
                for k in range(4):
                    a = k % 2
                    T["var_ready"].wait(pool, k + 1, t)
                    nc.gpsimd.tensor_tensor(sd[a][:], mv[a][:, :, 1], half[:], ALU.pow).then_inc(sems["sd_ready"], 1)

        @block.tensor
        def _(pe):
            pe.wait_ge(s_const, 48)
            for l2, lp, p, t in turns(pe):
                T = tallies()
                for x in T.values():
                    x.turn(t)
                wq, wk, wv, wo = (wqkvo[lp][:, i] for i in range(4))

                def transposed(a, name, src, ready, n):
                    g = acquire(pe, t, (a, name, 0))
                    T[ready].wait(pe, n)
                    for k in range(KD):
                        for i in range(NT):
                            last = pe.transpose(g[:, k * S + i * P:k * S + i * P + P],
                                                src[:, i, k * P:(k + 1) * P], ident[:])
                    filled(last, (a, name, 0))

                def feature_major(a, name, w):
                    g = acquire(pe, t, (a, name, 0))
                    for m in range(KD):
                        for k in range(KD):
                            last = pe.matmul(g[:, m * S:(m + 1) * S], w[:, k, m * P:(m + 1) * P],
                                             yT[a][:, k, :], start=(k == 0), stop=(k == KD - 1))
                    filled(last, (a, name, 0))

                def token_major(a, name, src, w, kt):
                    g = acquire(pe, t, (a, name, 0))
                    for i in range(NT):
                        for k in range(kt):
                            last = pe.matmul(g[:, i * D:(i + 1) * D], src[:, k, i * P:(i + 1) * P],
                                             w[:, k, :], start=(k == 0), stop=(k == kt - 1))
                    filled(last, (a, name, 0))

                def scores(grp):
                    a = grp // 4
                    if grp % 4 == 0:
                        evacuated(pe, t, (a, "q", 0))
                        evacuated(pe, t, (a, "k", 0))
                    qt, c = (grp % 4) // 2, grp % 2
                    units = [(a, "S", 4 * (grp % 4) + j) for j in range(4)]
                    gs = [acquire(pe, t, u) for u in units]
                    for odd in range(2):
                        for j in range(4):
                            r = slice(32 * j, 32 * j + 32)
                            last = pe.matmul(gs[j][:, odd * S:(odd + 1) * S],
                                             qm[a][r, odd, c, qt * P:(qt + 1) * P], kT[a][r, c, :],
                                             start=True, stop=True)
                            if odd:
                                filled(last, units[j])

                def turn_probs(u):
                    a, i = divmod(u, 16)
                    if u >= 2:
                        T["pt_dve" if u % 2 == 0 else "pt_act"].wait(pe, u // 2)
                    evacuated(pe, t, (a, "S", i))
                    for x in range(2):
                        for kb in range(NT):
                            last = pe.transpose(ptp[u % 2][:, x, kb, :], probs[u % 8][:, x, kb * P:(kb + 1) * P], ident[:])
                    last.then_inc(sems["pt_full"], 1)

                def pv(u):
                    a, i = divmod(u, 16)
                    if i == 0:
                        evacuated(pe, t, (a, "v", 0))
                    if u >= 30:
                        T["pt_dve" if u % 2 == 0 else "pt_act"].wait(pe, u // 2 + 1)
                    qt, c, j = i // 8, (i // 4) % 2, i % 4
                    out = ops[a][32 * j:32 * j + 32, c * S + qt * P:c * S + (qt + 1) * P]
                    for x in range(2):
                        for kb in range(NT):
                            last = pe.matmul(out, v[a][:, kb, 4 * c + j, x, :], pts[u % 4][:, x, kb, :],
                                             start=(x == 0 and kb == 0), stop=(x == 1 and kb == NT - 1))
                    if i == 15:
                        last.then_inc(sems["o_full"], 1)

                def ffn_up(a):
                    evacuated(pe, t, (a, "y2T", 0))
                    for i in range(4):
                        u = (a, "w1", i)
                        g = acquire(pe, t, u)
                        for m in range(2):
                            f = 2 * i + m
                            for k in range(KD):
                                last = pe.matmul(g[:, m * S:(m + 1) * S], w1[lp][:, k, f * P:(f + 1) * P],
                                                 yT[a][:, k, :], start=(k == 0), stop=(k == KD - 1))
                        filled(last, u)

                def ffn_down(a):
                    for i in range(4):
                        evacuated(pe, t, (a, "w1", i))
                    token_major(a, "w2", aT[a], w2[lp], FT)

                if True:
                    transposed(0, "yT", yn[0], "yn_ready", 1)
                    transposed(1, "yT", yn[1], "yn_ready", 2)
                    pe.wait_ge(s_w[lp], l2 * (16 * NLOAD) + 16 * NLOAD)
                    for a in range(2):
                        evacuated(pe, t, (a, "yT", 0))
                        feature_major(a, "q", wq)
                        feature_major(a, "k", wk)
                        token_major(a, "v", yT[a], wv, KD)
                    for grp in range(9):
                        if grp < 8:
                            scores(grp)
                        if grp == 7:
                            transposed(0, "rT", rb[0][:].rearrange("p i n d -> p i (n d)"), "rb_ready", 1)
                        if grp == 8:
                            T["oT_ready"].wait(pe, 1)
                            token_major(0, "wo", oT[0], wo, KD)
                        if grp >= 1:
                            for j in range(4):
                                u = 4 * (grp - 1) + j
                                turn_probs(u)
                                if u >= 2:
                                    pv(u - 2)
                    pv(30)
                    pv(31)
                    transposed(1, "rT", rb[1][:].rearrange("p i n d -> p i (n d)"), "rb_ready", 2)
                    transposed(0, "y2T", yn[0], "yn_ready", 3)
                    ffn_up(0)
                    T["oT_ready"].wait(pe, 2)
                    token_major(1, "wo", oT[1], wo, KD)
                    ffn_down(0)
                    transposed(1, "y2T", yn[1], "yn_ready", 4)
                    ffn_up(1)
                    ffn_down(1)

        @block.scalar
        def _(act):
            for l2, lp, p, t in turns(act):
                T = tallies()
                for x in T.values():
                    x.turn(t)

                def y_out(a, name, ln):
                    u = (a, name, 0)
                    g = take(act, t, u)
                    for k in range(KD):
                        last = nc.scalar.activation(yT[a][:, k, :], g[:, k * S:(k + 1) * S], ACT.Identity,
                                                    scale=cols[lp][:, C_LNA + 2 * ln + k:C_LNA + 2 * ln + k + 1],
                                                    bias=cols[lp][:, C_LNB + 2 * ln + k:C_LNB + 2 * ln + k + 1])
                    release(last, u)

                def exps(u):
                    a, i = divmod(u, 16)
                    un = (a, "S", i)
                    T["max_ready"].wait(act, u + 1)
                    g = bank[place[un][0]]
                    qt, c, j = i // 8, (i // 4) % 2, i % 4
                    for x in range(2):
                        col = qt * H + 8 * c + 2 * j + x
                        last = nc.scalar.activation(probs[u % 8][:, x, :], g[:, x * S:(x + 1) * S], ACT.Exp,
                                                    bias=nmax[a][:, col:col + 1], accum_out=rsum[a][:, col:col + 1])
                    release(last, un)

                def copy_pt(u):
                    T["pt_full"].wait(act, u + 1)
                    nc.scalar.activation(pts[u % 4][:], ptp[u % 2][:], ACT.Copy).then_inc(sems["pt_act"], 1)

                def r_out(a):
                    u = (a, "rT", 0)
                    g = take(act, t, u)
                    release(nc.scalar.activation(rT[a][:], g[:], ACT.Copy), u)

                def relu(a, i):
                    u = (a, "w1", i)
                    g = take(act, t, u)
                    for m in range(2):
                        f = 2 * i + m
                        last = nc.scalar.activation(aT[a][:, f, :], g[:, m * S:(m + 1) * S], ACT.Relu,
                                                    bias=cols[lp][:, C_B1 + f:C_B1 + f + 1])
                    release(last, u)

                if True:
                    act.wait_ge(s_w[lp], l2 * (16 * NLOAD) + 16 * NLOAD)
                    y_out(0, "yT", 0)
                    y_out(1, "yT", 0)
                    for a in range(2):
                        u = (a, "k", 0)
                        g = take(act, t, u)
                        for m in range(KD):
                            last = nc.scalar.activation(kT[a][:, m, :], g[:, m * S:(m + 1) * S], ACT.Identity,
                                                        bias=cols[lp][:, C_BK + m:C_BK + m + 1])
                        release(last, u)
                    for grp in range(9):
                        for j in range(4):
                            if grp < 8:
                                exps(4 * grp + j)
                            if grp == 7 and j == 1:
                                r_out(0)
                            if grp >= 1 and j % 2:
                                copy_pt(4 * (grp - 1) + j)
                    r_out(1)
                    y_out(0, "y2T", 1)
                    relu(0, 0)
                    relu(0, 1)
                    y_out(1, "y2T", 1)
                    relu(1, 0)
                    relu(1, 1)

        @block.vector
        def _(dve):
            for i in range(BANKS):
                nc.vector.memset(scratch[:, i:i + 1], 0.0).then_inc(s_free[i], 1)
            dve.wait_ge(s_idx, 16)
            step = sems["dve_step"]
            nc.vector.tensor_copy(idxf[:], idx[:]).then_inc(step, 1)
            dve.wait_ge(step, 1)
            nc.vector.tensor_scalar(idxn[:], idxf[:], 0.0, float(V), ALU.is_lt, ALU.mult).then_inc(step, 1)
            dve.wait_ge(step, 2)
            nc.vector.tensor_tensor(idxf[:], idxf[:], idxn[:], ALU.add).then_inc(step, 1)
            dve.wait_ge(step, 3)
            nc.vector.tensor_scalar(idxn[:], idxf[:], 0.0, float(V - 1), ALU.max, ALU.min).then_inc(step, 1)
            dve.wait_ge(step, 4)
            nc.vector.tensor_copy(idxu[:], idxn[:]).then_inc(s_idx, 1)
            dve.wait_ge(s_const, 48)
            for a in range(2):
                nc.vector.memset(v[a][:], 0.0).then_inc(step, 1)
            for s in range(B):
                dve.wait_ge(s_gather, 16 * NT * B)
                nc.vector.tensor_tensor(h[:, s], h[:, s], pe_sb[:], ALU.add).then_inc(step, 1)
            for l2, lp, p, t in turns(dve):
                T = tallies()
                for x in T.values():
                    x.turn(t)
                T["dve_step"].credit = FIRST
                chain = T["dve_step"]

                def link(ins):
                    chain.up(ins)

                def after():
                    chain.wait(dve)

                def after_held():
                    after()
                    link(nc.vector.memset(scratch[:, BANKS:], 0.0))

                def stats_of(a):
                    after_held()
                    for i in range(NT):
                        last = nc.vector.bn_stats(stats[a][:, i, :], h[:, 2 * p + a, i, :])
                    link(last)
                    after_held()
                    for i in range(NT):
                        last = nc.vector.bn_aggr(mv[a][:, i, :], stats[a][:, i, :])
                    last.then_inc(sems["var_ready"], 1)

                def normalise(a, k):
                    T["sd_ready"].credit = 1
                    T["sd_ready"].wait(dve, k)
                    link(nc.vector.tensor_scalar(den[a][:], sd[a][:], float((D / (D - 1)) ** 0.5), TOK_EPS, ALU.mult, ALU.add))
                    after()
                    link(nc.vector.reciprocal(rstd[a][:], den[a][:]))
                    after()
                    for i in range(NT):
                        last = nc.vector.tensor_scalar(yn[a][:, i, :], h[:, 2 * p + a, i, :], mv[a][:, i, 0:1],
                                                       rstd[a][:, i:i + 1], ALU.subtract, ALU.mult)
                    last.then_inc(sems["yn_ready"], 1)

                def q_out(a):
                    u = (a, "q", 0)
                    g = take(dve, t, u)
                    for odd in range(2):
                        for m in range(KD):
                            last = nc.vector.tensor_scalar(qm[a][:, odd, m, :], g[:, m * S:(m + 1) * S],
                                                           cols[lp][:, C_BQ + m:C_BQ + m + 1], qmask[:, odd:odd + 1],
                                                           ALU.add, ALU.mult)
                    release(last, u)

                def v_out(a):
                    u = (a, "v", 0)
                    g = take(dve, t, u)
                    gv = g[:].rearrange("p (i n x d) -> p i n x d", i=NT, x=2, d=DK)
                    bv = rows[lp][:, R_BV, :].rearrange("p (n x d) -> p n x d", x=2, d=DK)
                    for i in range(NT):
                        for x in range(2):
                            last = nc.vector.tensor_tensor(v[a][:, i, :, x, x * DK:(x + 1) * DK], gv[:, i, :, x, :],
                                                           bv[:, :, x, :], ALU.add)
                    release(last, u)

                def row_max(u):
                    a, i = divmod(u, 16)
                    g = take(dve, t, (a, "S", i))
                    qt, c, j = i // 8, (i // 4) % 2, i % 4
                    col = qt * H + 8 * c + 2 * j
                    nc.vector.tensor_reduce(nmax[a][:, col:col + 2], g[:].rearrange("p (x s) -> p x s", x=2),
                                            AX.X, ALU.max, negate=True).then_inc(sems["max_ready"], 1)

                def copy_pt(u):
                    T["pt_full"].wait(dve, u + 1)
                    nc.vector.tensor_copy(pts[u % 4][:], ptp[u % 2][:]).then_inc(sems["pt_dve"], 1)

                def recips(a):
                    evacuated(dve, t, (a, "S", 15))
                    link(nc.vector.reciprocal(rinv[a][:], rsum[a][:]))
                    after()
                    nc.vector.tensor_copy(rb[a][:], rinv[a][:].rearrange("p (i n x) -> p i n x", i=NT, x=1)
                                          .to_broadcast((P, NT, H, DK))).then_inc(sems["rb_ready"], 1)

                def o_norm(a):
                    evacuated(dve, t, (a, "rT", 0))
                    T["o_full"].wait(dve, a + 1)
                    nc.vector.tensor_tensor(oT[a][:].rearrange("p k s -> p (k s)"), ops[a][:],
                                            rT[a][:].rearrange("p k s -> p (k s)"), ALU.mult).then_inc(sems["oT_ready"], 1)

                def residual(a, name, row):
                    u = (a, name, 0)
                    g = take(dve, t, u)
                    ins = nc.vector.tensor_tensor(h[:, 2 * p + a], h[:, 2 * p + a], g[:].rearrange("p (i d) -> p i d", i=NT), ALU.add)
                    release(ins, u)
                    evacuated(dve, t, u)
                    return nc.vector.tensor_tensor(h[:, 2 * p + a], h[:, 2 * p + a],
                                                   rows[lp][:, row:row + 1, :].to_broadcast((P, NT, D)), ALU.add)

                def relu(a, i):
                    u = (a, "w1", i)
                    g = take(dve, t, u)
                    for m in range(2):
                        f = 2 * i + m
                        last = nc.vector.tensor_scalar(aT[a][:, f, :], g[:, m * S:(m + 1) * S],
                                                       cols[lp][:, C_B1 + f:C_B1 + f + 1], 0.0, ALU.add, ALU.max)
                    release(last, u)

                if True:
                    dve.wait_ge(s_w[lp], l2 * (16 * NLOAD) + 16 * NLOAD)
                    stats_of(0)
                    stats_of(1)
                    normalise(0, 1)
                    normalise(1, 2)
                    for a in range(2):
                        q_out(a)
                        v_out(a)
                    for grp in range(9):
                        for j in range(4):
                            if grp < 8:
                                row_max(4 * grp + j)
                            if grp >= 1 and j % 2:
                                copy_pt(4 * (grp - 1) + j - 1)
                        if grp == 5:
                            recips(0)
                        if grp == 7:
                            o_norm(0)
                    recips(1)
                    link(residual(0, "wo", R_BO))
                    stats_of(0)
                    normalise(0, 3)
                    o_norm(1)
                    relu(0, 2)
                    relu(0, 3)
                    link(residual(1, "wo", R_BO))
                    stats_of(1)
                    normalise(1, 4)
                    link(residual(0, "w2", R_B2))
                    relu(1, 2)
                    relu(1, 3)
                    link(residual(1, "w2", R_B2))
                    chain.whole()


def windowed_attention(nc, io, h, wqkv, wout, s_w2):
    ctx = ExitStack()
    with ctx:
        sb = lambda name, shape, dt=F32: ctx.enter_context(nc.sbuf_tensor(name, shape, dt))
        pb = lambda name, shape: ctx.enter_context(nc.psum_tensor(name, shape, F32))
        sem = lambda name: ctx.enter_context(nc.semaphore(name))

        ident = sb("w_ident", [P, P])
        mask = sb("mask", [P, 1, KEYS2])
        normab = sb("normab", [P, 2, D])
        gamma = sb("gamma", [P, KD])
        pmk = sb("pmk", [P, CT, 1, PM])
        pmv = sb("pmv", [PM, INNER])
        expo = sb("expo", [P, 2, NT])
        stats = [sb(f"w_stats{a}", [P, NT, 6]) for a in range(2)]
        mv = [sb(f"w_mv{a}", [P, NT, 2]) for a in range(2)]
        mv2 = [sb(f"w_mv2{a}", [P, NT, 2]) for a in range(2)]
        sd = [sb(f"w_sd{a}", [P, NT]) for a in range(2)]
        sd2 = [sb(f"w_sd2{a}", [P, NT]) for a in range(2)]
        den = [sb(f"w_den{a}", [P, NT]) for a in range(2)]
        rstd = [sb(f"w_rstd{a}", [P, NT]) for a in range(2)]
        yn = [sb(f"w_yn{a}", [P, NT, D]) for a in range(2)]
        yT = [sb(f"w_yT{a}", [P, KD, S]) for a in range(2)]
        qT = [sb(f"w_qT{a}", [P, CT, S]) for a in range(2)]
        kT = [sb(f"w_kT{a}", [P, CT, NT, KEYS2]) for a in range(2)]
        v = [sb(f"w_v{a}", [P, NT, INNER]) for a in range(2)]
        nmax = [sb(f"w_nmax{a}", [P, NT * HEADS2]) for a in range(2)]
        rsum = [sb(f"w_rsum{a}", [P, NT * HEADS2]) for a in range(2)]
        rinv = [sb(f"w_rinv{a}", [P, NT * HEADS2]) for a in range(2)]
        probs = [sb(f"w_probs{i}", [P, 2, KEYS2]) for i in range(8)]
        pts = [sb(f"w_pts{i}", [P, 2, 2, P]) for i in range(4)]
        rb = [sb(f"w_rb{i}", [P, 8, DH2]) for i in range(2)]
        rT = [sb(f"w_rT{i}", [P, 4, P]) for i in range(2)]
        oT = [sb(f"w_oT{a}", [P, CT, S]) for a in range(2)]
        scratch = sb("w_scratch", [P, BANKS + 1])
        bank = [pb(f"w_bank{i}", [P, 512]) for i in range(BANKS)]
        ptp = [pb(f"w_ptp{i}", [P, 2, 2, P]) for i in range(2)]
        ops = [pb(f"w_ops{i}", [P, 512]) for i in range(2)]

        order = [(a, "yT", 0) for a in (0, 1)]
        order += [(a, n, i) for a in (0, 1) for n in "qkv" for i in range(4)]
        for g in range(8):
            order += [(g // 4, "S", 4 * (g % 4) + j) for j in range(4)]
            if g == 7:
                order += [(0, "wo", 0)]
            if g >= 2:
                order += [((g - 2) // 4, "rT", (g - 2) % 4)]
        order += [(1, "rT", 2), (1, "rT", 3), (1, "wo", 0)]
        USES = len(order) // BANKS
        assert len(order) % BANKS == 0
        place = {u: (i % BANKS, i // BANKS) for i, u in enumerate(order)}

        s_const = sem("w_const")
        s_full = [sem(f"w_full{i}") for i in range(BANKS)]
        s_free = [sem(f"w_free{i}") for i in range(BANKS)]
        names = dict(yn_ready=2, max_ready=32, pt_full=32, pt_act=16, pt_dve=16, o_full=8,
                     rb_ready=8, oT_ready=8, var_ready=4, sd_ready=4, dve_step=66)
        sems = {n: sem("w_" + n) for n in names}
        FIRST = 1
        NCONST = 6

        def tallies(t):
            T = {n: Tally(sems[n], per) for n, per in names.items()}
            for x in T.values():
                x.turn(t)
            return T

        def acquire(pe, t, u):
            b, use = place[u]
            pe.wait_ge(s_free[b], t * USES + use + 1)
            return bank[b]

        def filled(ins, u):
            ins.then_inc(s_full[place[u][0]], 1)

        def take(eng, t, u):
            b, use = place[u]
            eng.wait_ge(s_full[b], t * USES + use + 1)
            return bank[b]

        def release(ins, u):
            ins.then_inc(s_free[place[u][0]], 1)

        def evacuated(eng, t, u):
            b, use = place[u]
            eng.wait_ge(s_free[b], t * USES + use + 2)

        block = ctx.enter_context(nc.Block())

        @block.sync
        def _(sp):
            for dst, src in ((ident[:], io["ident"]), (mask[:], io["mask"]), (normab[:], io["normab"].partition_broadcast(P)),
                             (gamma[:], io["gamma"]), (pmk[:], io["pmk"]), (pmv[:], io["pmv"])):
                sp.dma_start(dst, src).then_inc(s_const, 16)

        @block.gpsimd
        def _(pool):
            nc.gpsimd.memset(expo[:, 0, :], 0.5).then_inc(sems["sd_ready"], 1)
            nc.gpsimd.memset(expo[:, 1, :], -0.5).then_inc(sems["sd_ready"], 1)
            pool.wait_ge(sems["sd_ready"], 2)
            with pool.Fori(0, PAIRS) as t:
                T = tallies(t)
                for k in range(4):
                    a = k % 2
                    T["var_ready"].wait(pool, k + 1)
                    if k < 2:
                        ins = nc.gpsimd.tensor_tensor(sd[a][:], mv[a][:, :, 1], expo[:, 0, :], ALU.pow)
                    else:
                        ins = nc.gpsimd.tensor_tensor(sd2[a][:], den[a][:], expo[:, 1, :], ALU.pow)
                    ins.then_inc(sems["sd_ready"], 1)

        @block.tensor
        def _(pe):
            pe.wait_ge(s_const, 16 * NCONST)
            pe.wait_ge(s_w2, 32)
            with pe.Fori(0, PAIRS) as t:
                T = tallies(t)

                def y_T(a):
                    u = (a, "yT", 0)
                    g = acquire(pe, t, u)
                    T["yn_ready"].wait(pe, 1 + a)
                    for k in range(KD):
                        for i in range(NT):
                            last = pe.transpose(g[:, k * S + i * P:k * S + i * P + P],
                                                yn[a][:, i, k * P:(k + 1) * P], ident[:])
                    filled(last, u)

                def project(a):
                    evacuated(pe, t, (a, "yT", 0))
                    for n in range(2):
                        for i in range(4):
                            u = (a, "qk"[n], i)
                            g = acquire(pe, t, u)
                            for x in range(2):
                                m = n * CT + 2 * i + x
                                for k in range(KD):
                                    last = pe.matmul(g[:, x * S:(x + 1) * S], wqkv[:, k, m * P:(m + 1) * P],
                                                     yT[a][:, k, :], start=(k == 0), stop=(k == KD - 1))
                            filled(last, u)
                    for i in range(4):
                        w, n = divmod(i, 2)
                        u = (a, "v", i)
                        g = acquire(pe, t, u)
                        for k in range(KD):
                            last = pe.matmul(g[:], yT[a][:, k, w * P:(w + 1) * P],
                                             wqkv[:, k, 2 * INNER + n * 512:2 * INNER + (n + 1) * 512],
                                             start=(k == 0), stop=(k == KD - 1))
                        filled(last, u)

                def scores(grp):
                    a, w = grp // 4, (grp % 4) // 2
                    units = [(a, "S", 4 * (grp % 4) + j) for j in range(4)]
                    gs = [acquire(pe, t, u) for u in units]
                    for x in range(2):
                        for j in range(4):
                            c = 2 * (2 * (grp % 2) + j // 2) + x
                            r = slice(64 * (j % 2), 64 * (j % 2) + 64)
                            last = pe.matmul(gs[j][:, x * KEYS2:(x + 1) * KEYS2], qT[a][r, c, w * P:(w + 1) * P],
                                             kT[a][r, c, w, :], start=True, stop=True)
                            if x:
                                filled(last, units[j])

                def turn_probs(u):
                    a, i = divmod(u, 16)
                    if u >= 2:
                        T["pt_dve" if u % 2 == 0 else "pt_act"].wait(pe, u // 2)
                    evacuated(pe, t, (a, "S", i))
                    for x in range(2):
                        pe.transpose(ptp[u % 2][0:PM, x, 1, :], probs[u % 8][:, x, 0:PM], ident[:])
                        last = pe.transpose(ptp[u % 2][:, x, 0, :], probs[u % 8][:, x, PM:KEYS2], ident[:])
                    last.then_inc(sems["pt_full"], 1)

                def pv(u):
                    a, i = divmod(u, 16)
                    grp = u // 4
                    if u % 4 == 0 and grp >= 2:
                        T["oT_ready"].wait(pe, grp - 1)
                    if u >= 30:
                        T["pt_dve" if u % 2 == 0 else "pt_act"].wait(pe, u // 2 + 1)
                    w, j = (grp % 4) // 2, u % 4
                    for x in range(2):
                        hl = 4 * (j // 2) + 2 * x + j % 2
                        hd = 8 * (grp % 2) + hl
                        m = hl // 2
                        out = ops[grp % 2][64 * (j % 2):64 * (j % 2) + 64, m * P:(m + 1) * P]
                        pe.matmul(out, v[a][:, w, hd * DH2:(hd + 1) * DH2], pts[u % 4][:, x, 0, :], start=True, stop=False)
                        last = pe.matmul(out, pmv[:, hd * DH2:(hd + 1) * DH2], pts[u % 4][0:PM, x, 1, :], start=False, stop=True)
                    if j == 3:
                        last.then_inc(sems["o_full"], 1)

                def r_T(grp):
                    u = (grp // 4, "rT", grp % 4)
                    g = acquire(pe, t, u)
                    T["rb_ready"].wait(pe, grp + 1)
                    for m in range(4):
                        last = pe.transpose(g[:, m * P:(m + 1) * P], rb[grp % 2][:, 2 * m:2 * m + 2, :], ident[:])
                    filled(last, u)

                def project_out(a):
                    u = (a, "wo", 0)
                    g = acquire(pe, t, u)
                    T["oT_ready"].wait(pe, 4 * (a + 1))
                    for i in range(NT):
                        for k in range(CT):
                            last = pe.matmul(g[:, i * D:(i + 1) * D], oT[a][:, k, i * P:(i + 1) * P], wout[:, k, :],
                                             start=(k == 0), stop=(k == CT - 1))
                    filled(last, u)

                y_T(0)
                y_T(1)
                project(0)
                project(1)
                for grp in range(9):
                    if grp < 8:
                        scores(grp)
                    if grp == 7:
                        project_out(0)
                    if grp >= 2:
                        r_T(grp - 2)
                    if grp >= 1:
                        for j in range(4):
                            u = 4 * (grp - 1) + j
                            turn_probs(u)
                            if u >= 2:
                                pv(u - 2)
                pv(30)
                pv(31)
                r_T(7)
                project_out(1)

        @block.scalar
        def _(act):
            act.wait_ge(s_const, 16 * NCONST)
            with act.Fori(0, PAIRS) as t:
                T = tallies(t)

                def y_out(a):
                    u = (a, "yT", 0)
                    g = take(act, t, u)
                    for k in range(KD):
                        last = nc.scalar.activation(yT[a][:, k, :], g[:, k * S:(k + 1) * S], ACT.Copy, scale=gamma[:, k:k + 1])
                    release(last, u)

                def exps(u):
                    a, i = divmod(u, 16)
                    un = (a, "S", i)
                    T["max_ready"].wait(act, u + 1)
                    g = bank[place[un][0]]
                    base = (i // 2) * 4 + i % 2
                    for x in range(2):
                        col = base + 2 * x
                        last = nc.scalar.activation(probs[u % 8][:, x, :], g[:, x * KEYS2:(x + 1) * KEYS2], ACT.Exp,
                                                    bias=nmax[a][:, col:col + 1], accum_out=rsum[a][:, col:col + 1])
                    release(last, un)

                def copy_pt(u):
                    T["pt_full"].wait(act, u + 1)
                    nc.scalar.activation(pts[u % 4][0:PM, :, 1, :], ptp[u % 2][0:PM, :, 1, :], ACT.Copy)
                    nc.scalar.activation(pts[u % 4][:, :, 0, :], ptp[u % 2][:, :, 0, :], ACT.Copy).then_inc(sems["pt_act"], 1)

                def r_out(grp):
                    u = (grp // 4, "rT", grp % 4)
                    g = take(act, t, u)
                    release(nc.scalar.activation(rT[grp % 2][:], g[:].rearrange("p (m s) -> p m s", m=4), ACT.Copy), u)

                y_out(0)
                y_out(1)
                for a in range(2):
                    for i in range(4):
                        u = (a, "q", i)
                        g = take(act, t, u)
                        release(nc.scalar.activation(qT[a][:, 2 * i:2 * i + 2, :], g[:].rearrange("p (x s) -> p x s", x=2),
                                                     ACT.Copy, scale=float(DH2 ** -0.5)), u)
                    for i in range(2):
                        u = (a, "v", 2 * i)
                        g = take(act, t, u)
                        release(nc.scalar.activation(v[a][:, i, 0:512], g[:], ACT.Copy), u)
                for grp in range(9):
                    for j in range(4):
                        if grp < 8:
                            exps(4 * grp + j)
                        if grp >= 2 and j == 1:
                            r_out(grp - 2)
                        if grp >= 1 and j % 2:
                            copy_pt(4 * (grp - 1) + j)
                r_out(7)

        @block.vector
        def _(dve):
            for i in range(BANKS):
                nc.vector.memset(scratch[:, i:i + 1], 0.0).then_inc(s_free[i], 1)
            dve.wait_ge(s_const, 16 * NCONST)
            for a in range(2):
                last = nc.vector.tensor_copy(kT[a][:, :, 0, 0:PM], pmk[:, :, 0, :])
                last = nc.vector.tensor_copy(kT[a][:, :, 1, 0:PM], pmk[:, :, 0, :])
            last.then_inc(sems["dve_step"], 1)
            with dve.Fori(0, PAIRS) as t:
                T = tallies(t)
                chain = T["dve_step"]
                chain.credit = FIRST
                T["sd_ready"].credit = 2

                def link(ins):
                    chain.up(ins)

                def after():
                    chain.wait(dve)

                def after_held():
                    after()
                    link(nc.vector.memset(scratch[:, BANKS:], 0.0))

                def stats_of(a, mvs):
                    after_held()
                    for i in range(NT):
                        last = nc.vector.bn_stats(stats[a][:, i, :], h[:, 2 * t + a, i, :])
                    link(last)
                    after_held()
                    for i in range(NT):
                        last = nc.vector.bn_aggr(mvs[a][:, i, :], stats[a][:, i, :])
                    return last

                def encoder_norm(a):
                    T["sd_ready"].wait(dve, 1 + a)
                    link(nc.vector.tensor_scalar(den[a][:], sd[a][:], float((D / (D - 1)) ** 0.5), TOK_EPS, ALU.mult, ALU.add))
                    after()
                    link(nc.vector.reciprocal(rstd[a][:], den[a][:]))
                    after()
                    for i in range(NT):
                        last = nc.vector.tensor_scalar(h[:, 2 * t + a, i, :], h[:, 2 * t + a, i, :], mv[a][:, i, 0:1],
                                                       rstd[a][:, i:i + 1], ALU.subtract, ALU.mult)
                    link(last)
                    after()
                    link(nc.vector.tensor_tensor(h[:, 2 * t + a], h[:, 2 * t + a], normab[:, 0:1, :].to_broadcast((P, NT, D)), ALU.mult))
                    after()
                    link(nc.vector.tensor_tensor(h[:, 2 * t + a], h[:, 2 * t + a], normab[:, 1:2, :].to_broadcast((P, NT, D)), ALU.add))

                def norms(a):
                    link(stats_of(a, mv2))
                    after()
                    link(nc.vector.tensor_scalar(den[a][:], mv2[a][:, :, 1], LN_EPS, RMS_EPS, ALU.add, ALU.mult))
                    after()
                    nc.vector.tensor_tensor(den[a][:], den[a][:], mv2[a][:, :, 1], ALU.add).then_inc(sems["var_ready"], 1)

                def normalise(a):
                    T["sd_ready"].wait(dve, 3 + a)
                    for i in range(NT):
                        last = nc.vector.tensor_scalar(yn[a][:, i, :], h[:, 2 * t + a, i, :], mv2[a][:, i, 0:1],
                                                       sd2[a][:, i:i + 1], ALU.subtract, ALU.mult)
                    last.then_inc(sems["yn_ready"], 1)

                def mask_scores(u):
                    a, i = divmod(u, 16)
                    g = take(dve, t, (a, "S", i))
                    gv = g[:, 0:2 * KEYS2].rearrange("p (x s) -> p x s", x=2)
                    link(nc.vector.tensor_tensor(gv, gv, mask[:].to_broadcast((P, 2, KEYS2)), ALU.add))

                def row_max(u):
                    a, i = divmod(u, 16)
                    after()
                    g = bank[place[(a, "S", i)][0]]
                    base = (i // 2) * 4 + i % 2
                    nc.vector.tensor_reduce(nmax[a][:, base:base + 3:2], g[:, 0:2 * KEYS2].rearrange("p (x s) -> p x s", x=2),
                                            AX.X, ALU.max, negate=True).then_inc(sems["max_ready"], 1)

                def copy_pt(u):
                    T["pt_full"].wait(dve, u + 1)
                    nc.vector.tensor_copy(pts[u % 4][0:PM, :, 1, :], ptp[u % 2][0:PM, :, 1, :])
                    nc.vector.tensor_copy(pts[u % 4][:, :, 0, :], ptp[u % 2][:, :, 0, :]).then_inc(sems["pt_dve"], 1)

                def recips(grp):
                    a, i = grp // 4, grp % 4
                    evacuated(dve, t, (a, "S", 4 * i + 3))
                    link(nc.vector.reciprocal(rinv[a][:, 8 * i:8 * i + 8], rsum[a][:, 8 * i:8 * i + 8]))
                    after()
                    nc.vector.tensor_copy(rb[grp % 2][:], rinv[a][:, 8 * i:8 * i + 8].rearrange("p (n x) -> p n x", x=1)
                                          .to_broadcast((P, 8, DH2))).then_inc(sems["rb_ready"], 1)

                def o_norm(grp):
                    a, w, half = grp // 4, (grp % 4) // 2, grp % 2
                    evacuated(dve, t, (a, "rT", grp % 4))
                    T["o_full"].wait(dve, grp + 1)
                    nc.vector.tensor_tensor(oT[a][:, 4 * half:4 * half + 4, w * P:(w + 1) * P],
                                            ops[grp % 2][:].rearrange("p (m s) -> p m s", m=4), rT[grp % 2][:],
                                            ALU.mult).then_inc(sems["oT_ready"], 1)

                def residual(a):
                    u = (a, "wo", 0)
                    g = take(dve, t, u)
                    release(nc.vector.tensor_tensor(h[:, 2 * t + a], h[:, 2 * t + a], g[:].rearrange("p (i d) -> p i d", i=NT), ALU.add), u)

                for a in range(2):
                    stats_of(a, mv).then_inc(sems["var_ready"], 1)
                for a in range(2):
                    encoder_norm(a)
                for a in range(2):
                    norms(a)
                for a in range(2):
                    normalise(a)
                for a in range(2):
                    for i in range(4):
                        u = (a, "k", i)
                        g = take(dve, t, u)
                        release(nc.vector.tensor_copy(kT[a][:, 2 * i:2 * i + 2, :, PM:],
                                                      g[:].rearrange("p (x w s) -> p x w s", x=2, w=2)), u)
                    for i in range(2):
                        u = (a, "v", 2 * i + 1)
                        g = take(dve, t, u)
                        release(nc.vector.tensor_copy(v[a][:, i, 512:], g[:]), u)
                for grp in range(9):
                    for j in range(4):
                        if grp < 8:
                            mask_scores(4 * grp + j)
                            row_max(4 * grp + j)
                        if grp >= 1 and j % 2:
                            copy_pt(4 * (grp - 1) + j - 1)
                    if grp >= 2:
                        o_norm(grp - 2)
                    if grp >= 1:
                        recips(grp - 1)
                    if grp == 7:
                        residual(0)
                o_norm(7)
                residual(1)
                chain.whole()


class Ring:

    def __init__(self, banks, full, free, order):
        assert len(order) % len(banks) == 0
        self.banks, self.full, self.free = banks, full, free
        self.uses = len(order) // len(banks)
        self.place = {u: (i % len(banks), i // len(banks)) for i, u in enumerate(order)}

    def acquire(self, pe, t, u):
        b, use = self.place[u]
        pe.wait_ge(self.free[b], t * self.uses + use + 1)
        return self.banks[b]

    def filled(self, ins, u):
        ins.then_inc(self.full[self.place[u][0]], 1)

    def take(self, eng, t, u):
        b, use = self.place[u]
        eng.wait_ge(self.full[b], t * self.uses + use + 1)
        return self.banks[b]

    def release(self, ins, u):
        ins.then_inc(self.free[self.place[u][0]], 1)

    def evacuated(self, eng, t, u):
        b, use = self.place[u]
        eng.wait_ge(self.free[b], t * self.uses + use + 2)


class Chain:

    def __init__(self, eng, sem):
        self.eng, self.sem, self.n = eng, sem, 0

    def __call__(self, ins):
        ins.then_inc(self.sem, 1)
        self.n += 1
        self.eng.wait_ge(self.sem, self.n)


def mixture(nc, io, h):
    XS = nc.dram_tensor("expert_rows", [E * CAP, D], F32).ap()
    YS = nc.dram_tensor("expert_outs", [E * CAP + 1, D], F32).ap()
    T16 = B * NT
    with ExitStack() as ctx:
        sb = lambda name, shape, dt=F32: ctx.enter_context(nc.sbuf_tensor(name, shape, dt))
        x_all = sb("x_all", [P, T16, D])
        ident = sb("m_ident", [P, P])
        zeros = sb("zeros", [P, 4, D])
        wsel = [sb(f"wsel{k}", [P, T16]) for k in range(TOPK)]
        slot_u = [sb(f"slot_u{k}", [P, T16], U32) for k in range(TOPK)]
        s_zero = ctx.enter_context(nc.semaphore("m_zero"))
        with ExitStack() as c2:
            sb2 = lambda name, shape, dt=F32: c2.enter_context(nc.sbuf_tensor(name, shape, dt))
            xT = sb2("xT_all", [P, KD, N])
            shared = sb2("shared", [P, SHARED, 6 * HID])
            s_shared = c2.enter_context(nc.semaphore("m_shared"))
            keys = sb2("keys", [P, T16, E])
            pick = [sb2(f"pick{k}", [P, T16, E]) for k in range(TOPK)]
            gate(nc, io, h, x_all, xT, ident, zeros, XS, YS, s_zero, shared, s_shared, keys, pick, wsel)
            shared_and_slots(nc, io, h, xT, ident, shared, s_shared, keys, pick, slot_u)
        experts(nc, io, h, x_all, ident, XS, YS, s_zero, wsel, slot_u)


def gate(nc, io, h, x_all, xT, ident, zeros, XS, YS, s_zero, shared, s_shared, keys, pick, wsel):
    ctx = ExitStack()
    T16 = B * NT
    with ctx:
        sb = lambda name, shape, dt=F32: ctx.enter_context(nc.sbuf_tensor(name, shape, dt))
        sem = lambda name: ctx.enter_context(nc.semaphore(name))
        gw = sb("gw", [P, KD, E])
        gb = sb("gb", [P, 1, E])
        iota = sb("iota", [P, 1, E])
        expo = sb("g_expo", [P, NT])
        scratch = sb("g_scratch", [P, 8])
        xn = [sb(f"xn{a}", [P, NT, D]) for a in range(2)]
        xs = [sb(f"xs{a}", [P, KD, S]) for a in range(2)]
        stats = [sb(f"g_stats{a}", [P, NT, 6]) for a in range(2)]
        mv = [sb(f"g_mv{a}", [P, NT, 2]) for a in range(2)]
        ve = [sb(f"g_ve{a}", [P, NT]) for a in range(2)]
        rs = [sb(f"g_rs{a}", [P, NT]) for a in range(2)]
        logit = sb("logit", [P, T16, E])
        lmax = sb("lmax", [P, T16])
        lexp = sb("lexp", [P, T16, E])
        lsum = sb("lsum", [P, T16])
        score = sb("score", [P, T16, E])
        top = sb("top", [P, T16, 8])
        topi = sb("topi", [P, T16, 8], U32)
        topf = sb("topf", [P, T16, 8])
        work = sb("g_work", [P, T16, E])
        banks = [ctx.enter_context(nc.psum_tensor(f"g_bank{i}", [P, 512], F32)) for i in range(4)]
        ring = Ring(banks, [sem(f"g_full{i}") for i in range(4)], [sem(f"g_free{i}") for i in range(4)],
                    [(0, "xT"), (1, "xT"), (0, "lg"), (1, "lg")])
        s_const, s_var, s_sd, s_xn = sem("g_const"), sem("g_var"), sem("g_sd"), sem("g_xn")
        s_step, s_lexp, s_logits, s_lsub = sem("g_step"), sem("g_lexp"), sem("g_logits"), sem("g_lsub")
        PER, FIRST = 8, 0
        block = ctx.enter_context(nc.Block())

        @block.sync
        def _(sp):
            sp.dma_start(ident[:], io["ident"]).then_inc(s_const, 16)
            sp.dma_start(gw[:], io["gate_w"]).then_inc(s_const, 16)
            sp.dma_start(gb[:], io["gate_b"].partition_broadcast(P)).then_inc(s_const, 16)
            sp.dma_start(iota[:], io["iota"].partition_broadcast(P)).then_inc(s_const, 16)
            sp.dma_start(shared[:], io["shared"]).then_inc(s_shared, 16)
            sp.wait_ge(s_zero, 1)
            for r in range(0, E * CAP, 4 * P):
                sp.dma_start(XS[r:r + 4 * P, :].rearrange("(p r) d -> p r d", r=4), zeros[:]).then_inc(s_zero, 16)
            sp.dma_start(YS[E * CAP:, :], zeros[0:1, 0, :]).then_inc(s_zero, 16)

        @block.gpsimd
        def _(pool):
            nc.gpsimd.memset(zeros[:], 0.0).then_inc(s_zero, 1)
            nc.gpsimd.memset(expo[:], -0.5).then_inc(s_sd, 1)
            pool.wait_ge(s_sd, 1)
            with pool.Fori(0, PAIRS) as t:
                for a in range(2):
                    pool.wait_ge(s_var, 2 * t + a + 1)
                    nc.gpsimd.tensor_tensor(rs[a][:], ve[a][:], expo[:], ALU.pow).then_inc(s_sd, 1)

        @block.tensor
        def _(pe):
            pe.wait_ge(s_const, 64)
            with pe.Fori(0, PAIRS) as t:
                for a in range(2):
                    g = ring.acquire(pe, t, (a, "xT"))
                    pe.wait_ge(s_xn, 2 * t + a + 1)
                    for k in range(KD):
                        for i in range(NT):
                            last = pe.transpose(g[:, k * S + i * P:k * S + i * P + P], xn[a][:, i, k * P:(k + 1) * P], ident[:])
                    ring.filled(last, (a, "xT"))
                for a in range(2):
                    g = ring.acquire(pe, t, (a, "lg"))
                    ring.evacuated(pe, t, (a, "xT"))
                    for i in range(NT):
                        for k in range(KD):
                            last = pe.matmul(g[:, i * E:(i + 1) * E], xs[a][:, k, i * P:(i + 1) * P], gw[:, k, :],
                                             start=(k == 0), stop=(k == KD - 1))
                    ring.filled(last, (a, "lg"))

        @block.scalar
        def _(act):
            with act.Fori(0, PAIRS) as t:
                for a in range(2):
                    g = ring.take(act, t, (a, "xT"))
                    gv = g[:].rearrange("p (k s) -> p k s", k=KD)
                    nc.scalar.activation(xs[a][:], gv, ACT.Copy)
                    ring.release(nc.scalar.activation(xT[:, :, bass.ds((2 * t + a) * S, S)], gv, ACT.Copy), (a, "xT"))
            act.wait_ge(s_lsub, 1)
            nc.scalar.activation(lexp[:], work[:], ACT.Exp).then_inc(s_lexp, 1)

        @block.vector
        def _(dve):
            for i in range(4):
                nc.vector.memset(scratch[:, i:i + 1], 0.0).then_inc(ring.free[i], 1)
            nc.vector.memset(scratch[:, 6:7], 0.0).then_inc(s_step, 1)
            with dve.Fori(0, PAIRS) as t:
                n = 0

                def link(ins):
                    nonlocal n
                    ins.then_inc(s_step, 1)
                    n += 1

                def after():
                    dve.wait_ge(s_step, t * PER + n + 1)

                def after_held():
                    after()
                    link(nc.vector.memset(scratch[:, 6:7], 0.0))

                for a in range(2):
                    after_held()
                    for i in range(NT):
                        last = nc.vector.bn_stats(stats[a][:, i, :], h[:, 2 * t + a, i, :])
                    link(last)
                    after_held()
                    for i in range(NT):
                        last = nc.vector.bn_aggr(mv[a][:, i, :], stats[a][:, i, :])
                    link(last)
                    after()
                    nc.vector.tensor_scalar(ve[a][:], mv[a][:, :, 1], LN_EPS, None, ALU.add).then_inc(s_var, 1)
                for a in range(2):
                    dve.wait_ge(s_sd, 2 * t + a + 2)
                    for i in range(NT):
                        nc.vector.tensor_scalar(x_all[:, (2 * t + a) * NT + i, :], h[:, 2 * t + a, i, :], mv[a][:, i, 0:1],
                                                rs[a][:, i:i + 1], ALU.subtract, ALU.mult)
                    for i in range(NT):
                        last = nc.vector.tensor_scalar(xn[a][:, i, :], h[:, 2 * t + a, i, :], mv[a][:, i, 0:1],
                                                       rs[a][:, i:i + 1], ALU.subtract, ALU.mult)
                    last.then_inc(s_xn, 1)
                for a in range(2):
                    g = ring.take(dve, t, (a, "lg"))
                    ring.release(nc.vector.tensor_copy(logit[:, bass.ds((2 * t + a) * NT, NT), :],
                                                       g[:, 0:NT * E].rearrange("p (i e) -> p i e", i=NT)), (a, "lg"))
                assert n == PER, n
            for a in range(2):
                dve.wait_ge(ring.free[2 + a], PAIRS + 1)
            do = Chain(dve, s_logits)
            spread = lambda m: m[:].rearrange("p (t x) -> p t x", x=1).to_broadcast((P, T16, E))
            do(nc.vector.tensor_reduce(lmax[:], logit[:], AX.X, ALU.max))
            nc.vector.tensor_tensor(work[:], logit[:], spread(lmax), ALU.subtract).then_inc(s_lsub, 1)
            dve.wait_ge(s_const, 64)
            dve.wait_ge(s_lexp, 1)
            do(nc.vector.tensor_reduce(lsum[:], lexp[:], AX.X, ALU.add))
            do(nc.vector.reciprocal(lmax[:], lsum[:]))
            do(nc.vector.tensor_tensor(work[:], lexp[:], spread(lmax), ALU.mult))
            do(nc.vector.tensor_tensor(score[:], work[:], gb[:].to_broadcast((P, T16, E)), ALU.add))
            for i in range(T16):
                last = nc.vector.max(top[:, i, :], score[:, i, :])
            do(last)
            for i in range(T16):
                last = nc.vector.max_index(topi[:, i, :], top[:, i, :], score[:, i, :])
            do(last)
            do(nc.vector.tensor_copy(topf[:], topi[:]))
            for k in range(TOPK):
                do(nc.vector.tensor_tensor(pick[k][:], iota[:].to_broadcast((P, T16, E)),
                                           topf[:, :, k:k + 1].to_broadcast((P, T16, E)), ALU.is_equal))
                do(nc.vector.tensor_tensor(work[:], pick[k][:], logit[:], ALU.mult))
                do(nc.vector.tensor_reduce(wsel[k][:], work[:], AX.X, ALU.add))
            do(nc.vector.tensor_tensor(score[:], pick[0][:], pick[1][:], ALU.add))
            do(nc.vector.tensor_tensor(work[:], score[:], logit[:], ALU.mult))
            do(nc.vector.tensor_scalar(lexp[:], score[:], 1.0, -NEG, ALU.subtract, ALU.mult))
            do(nc.vector.tensor_tensor(keys[:], work[:], lexp[:], ALU.add))


def shared_and_slots(nc, io, h, xT, ident, shared, s_shared, keys, pick, slot_u):
    ctx = ExitStack()
    T16 = B * NT
    STEPS = 32
    with ctx:
        sb = lambda name, shape, dt=F32: ctx.enter_context(nc.sbuf_tensor(name, shape, dt))
        sem = lambda name: ctx.enter_context(nc.semaphore(name))
        same = sb("same", [P, P])
        before = sb("before", [P, P])
        bits = sb("bits", [P, STEPS + 1], I32)
        base = sb("base", [P, 1])
        ones = sb("ones", [P, P])
        kT = sb("keysT", [P, 2, P])
        junk = sb("junk", [P, 2, P])
        found = sb("found", [P, 1], I32)
        trial = sb("trial", [P, 1], I32)
        passed = sb("passed", [P, 1], I32)
        cnt = sb("cnt", [P, 1])
        gt = sb("gt", [P, 2, P])
        eq = sb("eq", [P, 2, P])
        run = sb("run", [P, 2, P])
        tot = sb("tot", [P, 2])
        off = sb("off", [P, 2])
        need = sb("need", [P, 1])
        asg = sb("asg", [P, 2, P])
        keep = sb("keep", [P, 2, P])
        slots = sb("slots", [P, 2, P])
        slotm = sb("slotm", [P, T16, E])
        work = sb("s_work", [P, T16, E])
        slotf = sb("slotf", [P, T16])
        w1 = [shared[:, e, 0:KD * HID].rearrange("p (k n) -> p k n", k=KD) for e in range(SHARED)]
        w3 = [shared[:, e, KD * HID:2 * KD * HID].rearrange("p (k n) -> p k n", k=KD) for e in range(SHARED)]
        w2 = [shared[:, e, 2 * KD * HID:].rearrange("p (k n) -> p k n", k=HT) for e in range(SHARED)]
        silu = [sb(f"silu{i}", [P, S]) for i in range(4)]
        gT = [sb(f"gT{a}", [P, SHARED * HT, S]) for a in range(2)]
        scratch = sb("s_scratch", [P, 8])
        NB = 6
        banks = [ctx.enter_context(nc.psum_tensor(f"s_bank{i}", [P, 512], F32)) for i in range(NB)]
        sps = ctx.enter_context(nc.psum_tensor("sps", [P, 512], F32))
        UP = SHARED * HT
        order = [(a, "up", i) for a in (0, 1) for i in range(UP)] + [(0, "down", 0), (1, "down", 0)]
        ring = Ring(banks, [sem(f"s_full{i}") for i in range(NB)], [sem(f"s_free{i}") for i in range(NB)], order)
        s_const, s_keysT, s_cnt, s_tot, s_step, s_silu = (sem(n) for n in
            ("s_const2", "s_keysT", "s_cnt", "s_tot", "s_step2", "s_silu"))
        s_tail, s_off = sem("s_tail"), sem("s_off")
        PER_TURN = STEPS // PAIRS
        block = ctx.enter_context(nc.Block())

        @block.sync
        def _(sp):
            for dst, src in ((same, "same"), (before, "before"), (bits, "bits"), (base, "base")):
                sp.dma_start(dst[:], io[src]).then_inc(s_const, 16)

        @block.tensor
        def _(pe):
            kv = keys[:].rearrange("p (x t) e -> p x (t e)", x=2)
            for x in range(2):
                last = pe.transpose(sps[:, x * P:(x + 1) * P], kv[:, x, :], ident[:])
            last.then_inc(s_keysT, 1)
            pe.wait_ge(s_const, 64)
            pe.wait_ge(s_shared, 16)
            with pe.Fori(0, PAIRS) as t:
                step = 0
                for a in range(2):
                    for i in range(UP):
                        u = (a, "up", i)
                        e, m = divmod(i, HT)
                        g = ring.acquire(pe, t, u)
                        for x, w in ((0, w1), (1, w3)):
                            for k in range(KD):
                                last = pe.matmul(g[:, x * S:(x + 1) * S], w[e][:, k, m * P:(m + 1) * P],
                                                 xT[:, k, bass.ds((2 * t + a) * S, S)],
                                                 start=(k == 0), stop=(k == KD - 1))
                        ring.filled(last, u)
                        if i % 2:
                            step += 1
                            pe.wait_ge(s_cnt, t * PER_TURN + step)
                            pe.matmul(sps[:, 0:1], same[:], cnt[:], start=True, stop=True).then_inc(s_tot, 1)
                for a in range(2):
                    u = (a, "down", 0)
                    g = ring.acquire(pe, t, u)
                    ring.evacuated(pe, t, (a, "up", UP - 1))
                    for i in range(NT):
                        for k in range(UP):
                            e, m = divmod(k, HT)
                            last = pe.matmul(g[:, i * D:(i + 1) * D], gT[a][:, k, i * P:(i + 1) * P], w2[e][:, m, :],
                                             start=(k == 0), stop=(k == UP - 1))
                    ring.filled(last, u)
            pe.wait_ge(s_tail, 1)
            pe.matmul(sps[:, 0:1], same[:], cnt[:], start=True, stop=True).then_inc(s_off, 1)
            for r in range(2):
                pe.wait_ge(s_tail, 2 + r)
                pe.matmul(sps[:, 0:2], before[:], tot[:], start=True, stop=True)
                pe.matmul(sps[:, 2:3], same[:], tot[:, 0:1], start=True, stop=True).then_inc(s_off, 1)
            pe.wait_ge(s_tail, 4)
            for x in range(2):
                last = pe.transpose(sps[:, x * P:(x + 1) * P], slots[:, x, :], ident[:])
            last.then_inc(s_off, 1)

        @block.scalar
        def _(act):
            with act.Fori(0, PAIRS) as t:
                for a in range(2):
                    for i in range(UP):
                        n = a * UP + i
                        g = ring.take(act, t, (a, "up", i))
                        if n >= 4:
                            prev = (n - 4) // UP, "up", (n - 4) % UP
                            ring.evacuated(act, t, prev)
                        nc.scalar.activation(silu[n % 4][:], g[:, 0:S], ACT.Silu).then_inc(s_silu, 1)

        @block.vector
        def _(dve):
            for i in range(NB):
                nc.vector.memset(scratch[:, i:i + 1], 0.0).then_inc(ring.free[i], 1)
            do = Chain(dve, s_step)
            nc.vector.memset(ones[:], 1.0)
            dve.wait_ge(s_const, 64)
            do(nc.vector.memset(found[:], -1))
            dve.wait_ge(s_keysT, 1)
            do(nc.vector.tensor_copy(kT[:], sps[:, 0:2 * P].rearrange("p (x s) -> p x s", x=2)))

            def count(cmp, out, **kw):
                return nc.vector.tensor_scalar(out[:], kT[:], trial[:].bitcast(F32), None, cmp, ALU.add, accum_out=cnt[:])

            do(nc.vector.tensor_tensor(trial[:], found[:], bits[:, 0:1], ALU.bitwise_xor))
            count(ALU.is_ge, junk).then_inc(s_cnt, 1)
            FIRST = do.n
            LINKS = 3
            with dve.Fori(0, PAIRS) as t:
                step = 0
                for a in range(2):
                    for i in range(UP):
                        u = (a, "up", i)
                        dve.wait_ge(s_silu, t * (2 * UP) + a * UP + i + 1)
                        g = ring.banks[ring.place[u][0]]
                        ring.release(nc.vector.tensor_tensor(gT[a][:, i, :], g[:, S:2 * S], silu[(a * UP + i) % 4][:], ALU.mult), u)
                        if i % 2:
                            at = t * PER_TURN + step
                            links = FIRST + at * LINKS
                            step += 1
                            dve.wait_ge(s_tot, t * PER_TURN + step)
                            nc.vector.tensor_scalar(passed[:], sps[:, 0:1], float(CAP) - 0.5, -1.0, ALU.is_gt, ALU.mult).then_inc(s_step, 1)
                            dve.wait_ge(s_step, links + 1)
                            nc.vector.scalar_tensor_tensor(out=found[:], in0=bits[:, bass.ds(at, 1)], scalar=passed[:],
                                                           in1=found[:], op0=ALU.bitwise_and, op1=ALU.bitwise_xor).then_inc(s_step, 1)
                            dve.wait_ge(s_step, links + 2)
                            nc.vector.tensor_tensor(trial[:], found[:], bits[:, bass.ds(at + 1, 1)], ALU.bitwise_xor).then_inc(s_step, 1)
                            dve.wait_ge(s_step, links + 3)
                            count(ALU.is_ge, junk).then_inc(s_cnt, 1)
                for a in range(2):
                    u = (a, "down", 0)
                    g = ring.take(dve, t, u)
                    ring.release(nc.vector.scalar_tensor_tensor(out=h[:, 2 * t + a], in0=g[:].rearrange("p (i d) -> p i d", i=NT),
                                                                scalar=1.0 / SHARED, in1=h[:, 2 * t + a], op0=ALU.mult, op1=ALU.add), u)
            do.n = FIRST + STEPS * LINKS
            dve.wait_ge(s_step, do.n)
            dve.wait_ge(s_cnt, STEPS + 1)
            nc.vector.tensor_scalar(gt[:], kT[:], found[:].bitcast(F32), None, ALU.is_gt, ALU.add, accum_out=cnt[:]).then_inc(s_tail, 1)
            do(nc.vector.tensor_scalar(eq[:], kT[:], found[:].bitcast(F32), None, ALU.is_equal))
            do(nc.vector.tensor_scalar(asg[:], kT[:], NEG, None, ALU.is_gt))
            dve.wait_ge(s_off, 1)
            do(nc.vector.tensor_scalar(need[:], sps[:, 0:1], -1.0, float(CAP), ALU.mult, ALU.add))

            def ranks(src, n):
                for x in range(2):
                    last = nc.vector.tensor_tensor_scan(run[:, x, :], ones[:], src[:, x, :], 0.0, ALU.mult, ALU.add)
                do(last)
                nc.vector.tensor_copy(tot[:], run[:, :, P - 1]).then_inc(s_tail, 1)
                dve.wait_ge(s_off, 2 + n)
                do(nc.vector.tensor_copy(off[:, 0:2], sps[:, 0:2]))
                do(nc.vector.tensor_tensor(off[:, 1:2], off[:, 1:2], sps[:, 2:3], ALU.add))

            ranks(eq, 0)
            for x in range(2):
                last = nc.vector.tensor_scalar(run[:, x, :], run[:, x, :], off[:, x:x + 1], need[:, 0:1], ALU.add, ALU.is_le)
            do(last)
            do(nc.vector.tensor_tensor(eq[:], eq[:], run[:], ALU.mult))
            do(nc.vector.tensor_tensor(keep[:], gt[:], eq[:], ALU.add))
            do(nc.vector.tensor_tensor(keep[:], keep[:], asg[:], ALU.mult))
            ranks(keep, 1)
            for x in range(2):
                last = nc.vector.tensor_scalar(run[:, x, :], run[:, x, :], off[:, x:x + 1], base[:, 0:1], ALU.add, ALU.add)
            do(last)
            do(nc.vector.tensor_tensor(run[:], run[:], keep[:], ALU.mult))
            nc.vector.tensor_scalar(slots[:], run[:], float(E * CAP), None, ALU.add).then_inc(s_tail, 1)
            dve.wait_ge(s_off, 4)
            do(nc.vector.tensor_copy(slotm[:], sps[:, 0:2 * P].rearrange("p (t e) -> p t e", e=E)))
            for k in range(TOPK):
                do(nc.vector.tensor_tensor(work[:], slotm[:], pick[k][:], ALU.mult))
                do(nc.vector.tensor_reduce(slotf[:], work[:], AX.X, ALU.add))
                do(nc.vector.tensor_copy(slot_u[k][:], slotf[:]))


def experts(nc, io, h, x_all, ident, XS, YS, s_zero, wsel, slot_u):
    ctx = ExitStack()
    T16 = B * NT
    RT = -(-CAP // P)
    ROWS = [min(P, CAP - i * P) for i in range(RT)]
    FULL = CAP // P
    with ctx:
        sb = lambda name, shape, dt=F32: ctx.enter_context(nc.sbuf_tensor(name, shape, dt))
        sem = lambda name: ctx.enter_context(nc.semaphore(name))
        we = [sb(f"we{a}", [P, 6 * HID]) for a in range(2)]
        w1 = [w[:, 0:KD * HID].rearrange("p (k n) -> p k n", k=KD) for w in we]
        w3 = [w[:, KD * HID:2 * KD * HID].rearrange("p (k n) -> p k n", k=KD) for w in we]
        w2 = [w[:, 2 * KD * HID:].rearrange("p (k n) -> p k n", k=HT) for w in we]
        rows = [sb(f"xrows{a}", [P, RT, D]) for a in range(2)]
        xeT = [sb(f"xeT{a}", [P, KD, CAP]) for a in range(2)]
        silu = [sb(f"e_silu{i}", [P, CAP]) for i in range(4)]
        gT = [sb(f"e_gT{a}", [P, HT, CAP]) for a in range(2)]
        ye = [sb(f"ye{a}", [P, RT, D]) for a in range(2)]
        back = [sb(f"back{k}", [P, T16, D]) for k in range(TOPK)]
        scratch = sb("e_scratch", [P, 9])
        NB = 8
        banks = [ctx.enter_context(nc.psum_tensor(f"e_bank{i}", [P, 512], F32)) for i in range(NB)]
        order = [(a, "xT", k) for a in (0, 1) for k in range(KD)]
        order += [(a, "up", i) for a in (0, 1) for i in range(2 * HT)]
        order += [(a, "down", i) for a in (0, 1) for i in range(2)]
        ring = Ring(banks, [sem(f"e_full{i}") for i in range(NB)], [sem(f"e_free{i}") for i in range(NB)], order)
        s_scat, s_stored, s_acc, s_out = (sem("e_" + n) for n in ("scat", "stored", "acc", "out"))
        s_we = [sem(f"e_we{a}") for a in range(2)]
        s_rows = [sem(f"e_rows{a}") for a in range(2)]
        s_back = [sem(f"e_back{s}") for s in range(B)]
        block = ctx.enter_context(nc.Block())

        @block.sync
        def _(sp):
            def load(e, a):
                sp.dma_start(we[a][:], io["experts"][e].rearrange("e p n -> p (e n)")).then_inc(s_we[a], 16)
                src = XS.rearrange("(e r) d -> e r d", e=E)[e]
                sp.dma_start(rows[a][:, 0:FULL, :], src[:, 0:FULL * P, :].rearrange("e (i p) d -> p (e i) d", p=P)).then_inc(s_rows[a], 16)
                sp.dma_start(rows[a][0:ROWS[-1], FULL, :], src[:, FULL * P:, :].rearrange("e r d -> (e r) d")).then_inc(s_rows[a], 16)

            sp.wait_ge(s_scat, 16 * TOPK * T16)
            for a in range(2):
                load(slice(a, a + 1), a)
            with sp.Fori(1, E // 2) as t:
                for a in range(2):
                    ring.take(sp, t - 1, (a, "down", 1))
                    load(bass.ds(2 * t + a, 1), a)

        @block.gpsimd
        def _(pool):
            pool.wait_ge(s_zero, 1 + 16 * (E * CAP // (4 * P) + 1))
            for j in range(T16):
                for k in range(TOPK):
                    pool.indirect_dma_start(XS, bass.IndirectOffsetOnAxis(ap=slot_u[k][:, j:j + 1], axis=0), x_all[:, j, :], None,
                                            bounds_check=E * CAP - 1, oob_is_err=False).then_inc(s_scat, 16)
            pool.wait_ge(s_stored, 1 + 2 * 16 * E)
            for j in range(T16):
                for k in range(TOPK):
                    pool.indirect_dma_start(back[k][:, j, :], None, YS,
                                            bass.IndirectOffsetOnAxis(ap=slot_u[k][:, j:j + 1], axis=0)).then_inc(s_back[j // NT], 16)

        @block.tensor
        def _(pe):
            with pe.Fori(0, E // 2) as t:
                for a in range(2):
                    pe.wait_ge(s_rows[a], t * 32 + 32)
                    for k in range(KD):
                        u = (a, "xT", k)
                        g = ring.acquire(pe, t, u)
                        for i in range(RT):
                            last = pe.transpose(g[:, i * P:i * P + ROWS[i]], rows[a][0:ROWS[i], i, k * P:(k + 1) * P],
                                                ident[0:ROWS[i], 0:ROWS[i]])
                        ring.filled(last, u)
                for a in range(2):
                    pe.wait_ge(s_we[a], t * 16 + 16)
                    for k in range(KD):
                        ring.evacuated(pe, t, (a, "xT", k))
                    for i in range(2 * HT):
                        m, x = divmod(i, 2)
                        u = (a, "up", i)
                        g = ring.acquire(pe, t, u)
                        for k in range(KD):
                            last = pe.matmul(g[:, 0:CAP], (w1, w3)[x][a][:, k, m * P:(m + 1) * P], xeT[a][:, k, :],
                                             start=(k == 0), stop=(k == KD - 1))
                        ring.filled(last, u)
                for a in range(2):
                    ring.evacuated(pe, t, (a, "up", 2 * HT - 1))
                    for half in range(2):
                        u = (a, "down", half)
                        g = ring.acquire(pe, t, u)
                        for i in ((0, 1) if half == 0 else (2,)):
                            for k in range(HT):
                                last = pe.matmul(g[0:ROWS[i], (i % 2) * D:(i % 2 + 1) * D], gT[a][:, k, i * P:i * P + ROWS[i]],
                                                 w2[a][:, k, :], start=(k == 0), stop=(k == HT - 1))
                        ring.filled(last, u)

        @block.scalar
        def _(act):
            with act.Fori(0, E // 2) as t:
                for a in range(2):
                    u = (a, "xT", 0)
                    g = ring.take(act, t, u)
                    ring.release(nc.scalar.activation(xeT[a][:, 0, :], g[:, 0:CAP], ACT.Copy), u)
                for a in range(2):
                    for m in range(HT):
                        n = a * HT + m
                        u = (a, "up", 2 * m)
                        g = ring.take(act, t, u)
                        if n >= 4:
                            ring.evacuated(act, t, ((n - 4) // HT, "up", 2 * ((n - 4) % HT) + 1))
                        ring.release(nc.scalar.activation(silu[n % 4][:], g[:, 0:CAP], ACT.Silu), u)
                for a in range(2):
                    e = 2 * t + a
                    dst = YS[0:E * CAP, :].rearrange("(e r) d -> e r d", e=E)[bass.ds(e, 1)]
                    ring.evacuated(act, t, (a, "down", 1))
                    act.dma_start(dst[:, 0:FULL * P, :].rearrange("e (i p) d -> p (e i) d", p=P), ye[a][:, 0:FULL, :]).then_inc(s_stored, 16)
                    act.dma_start(dst[:, FULL * P:, :].rearrange("e r d -> (e r) d"), ye[a][0:ROWS[-1], FULL, :]).then_inc(s_stored, 16)
            for s in range(B):
                act.wait_ge(s_acc, 2 * s + 2)
                act.dma_start(io["out"].rearrange("(s i p) d -> s p i d", p=P, i=NT)[s], h[:, s]).then_inc(s_out, 16)
            act.wait_ge(s_out, 16 * B)

        @block.vector
        def _(dve):
            for i in range(NB):
                nc.vector.memset(scratch[:, i:i + 1], 0.0).then_inc(ring.free[i], 1)
            nc.vector.memset(scratch[:, NB:NB + 1], 0.0).then_inc(s_stored, 1)
            with dve.Fori(0, E // 2) as t:
                for a in range(2):
                    u = (a, "xT", 1)
                    g = ring.take(dve, t, u)
                    ring.release(nc.vector.tensor_copy(xeT[a][:, 1, :], g[:, 0:CAP]), u)
                for a in range(2):
                    for m in range(HT):
                        u = (a, "up", 2 * m + 1)
                        ring.evacuated(dve, t, (a, "up", 2 * m))
                        g = ring.take(dve, t, u)
                        ring.release(nc.vector.tensor_tensor(gT[a][:, m, :], g[:, 0:CAP], silu[(a * HT + m) % 4][:], ALU.mult), u)
                for a in range(2):
                    u = (a, "down", 0)
                    g = ring.take(dve, t, u)
                    dve.wait_ge(s_stored, t * 64 + 1)
                    ring.release(nc.vector.tensor_copy(ye[a][:, 0:FULL, :], g[:].rearrange("p (i d) -> p i d", i=2)), u)
                    u = (a, "down", 1)
                    g = ring.take(dve, t, u)
                    ring.release(nc.vector.tensor_copy(ye[a][0:ROWS[-1], FULL, :], g[0:ROWS[-1], 0:D]), u)
            for s in range(B):
                dve.wait_ge(s_back[s], 16 * NT * TOPK)
                for k in range(TOPK):
                    if k:
                        dve.wait_ge(s_acc, 2 * s + 1)
                    for i in range(NT):
                        j = s * NT + i
                        last = nc.vector.scalar_tensor_tensor(out=h[:, s, i, :], in0=back[k][:, j, :], scalar=wsel[k][:, j:j + 1],
                                                              in1=h[:, s, i, :], op0=ALU.mult, op1=ALU.add)
                    last.then_inc(s_acc, 1)


def build(nc, io):
    with ExitStack() as ctx:
        sb = lambda name, shape: ctx.enter_context(nc.sbuf_tensor(name, shape, F32))
        h = sb("h", [P, B, NT, D])
        with ExitStack() as c2:
            wqkv = c2.enter_context(nc.sbuf_tensor("wqkv", [P, KD, 3 * INNER], F32))
            wout = c2.enter_context(nc.sbuf_tensor("wout", [P, CT, D], F32))
            s_w2 = c2.enter_context(nc.semaphore("s_w2"))
            embed_and_encoder(nc, io, h, wqkv, wout, s_w2)
            windowed_attention(nc, io, h, wqkv, wout, s_w2)
        mixture(nc, io, h)


def layout(x):
    g = {k: np.asarray(a) for k, a in x.items()}
    cut = lambda w: w.reshape(*w.shape[:-2], w.shape[-2] // P, P, w.shape[-1]).swapaxes(-3, -2)
    flat = lambda w: np.ascontiguousarray(w).reshape(*w.shape[:-2], -1)
    t = {}
    t["idx"] = g["x"].reshape(B, NT, P).transpose(2, 0, 1).reshape(P, B * NT)
    t["emb"] = g["L0_tok_emb"]
    aw, w1, w2 = cut(g["L0_tok_attn_w"]), cut(g["L0_tok_w1"]), cut(g["L0_tok_w2"])
    t["wtok"] = np.concatenate([aw.transpose(0, 2, 1, 3, 4).reshape(L, P, -1),
                                w1.reshape(L, P, -1), w2.reshape(L, P, -1)], axis=2)
    col = lambda w: w.reshape(L, -1, P).transpose(0, 2, 1)
    ab = g["L0_tok_attn_b"]
    t["cols"] = np.concatenate([col(g["L0_tok_ln_a"]), col(g["L0_tok_ln_b"]), col(ab[:, 0]), col(ab[:, 1]),
                                col(g["L0_tok_b1"])], axis=2)
    t["rows"] = np.stack([ab[:, 2], ab[:, 3], g["L0_tok_b2"]], axis=1)
    pos = np.arange(S, dtype=np.float32)[:, None]
    div = np.exp(np.arange(0, D, 2, dtype=np.float32) * -(np.log(10000.0) / D))
    pe = np.zeros((S, D), np.float32)
    pe[:, 0::2], pe[:, 1::2] = np.sin(pos * div), np.cos(pos * div)
    t["pe"] = pe.reshape(NT, P, D).transpose(1, 0, 2)
    t["ident"] = np.eye(P, dtype=np.float32)
    even = (np.arange(P) // DK) % 2 == 0
    t["qmask"] = np.stack([even, ~even], 1).astype(np.float32) * np.float32(DK ** -0.5)
    t["wqkv"], t["wout"] = cut(g["L0_attn_w_qkv"]), cut(g["L0_attn_w_out"])
    t["gamma"] = g["L0_attn_gamma"].reshape(KD, P).T
    t["normab"] = np.stack([g["L0_tok_norm_a"], g["L0_tok_norm_b"]])
    t["pmk"] = g["L0_attn_pm_k"].reshape(CT, 2, PM, DH2).transpose(1, 3, 0, 2).reshape(P, CT, 1, PM)
    t["pmv"] = g["L0_attn_pm_v"].transpose(1, 0, 2).reshape(PM, INNER)
    ex = lambda p: [cut(g[f"L0_ffn_{p}w{i}"]) for i in (1, 3, 2)]
    t["experts"] = np.concatenate([w.reshape(E, P, -1) for w in ex("e")], axis=2)
    t["shared"] = np.concatenate([w.reshape(SHARED, P, -1) for w in ex("s")], axis=2).transpose(1, 0, 2)
    t["gate_w"], t["gate_b"] = cut(g["L0_ffn_gate_w"]), g["L0_ffn_gate_b"].reshape(1, E)
    t["iota"] = np.arange(E, dtype=np.float32).reshape(1, E)
    e, t8 = np.arange(P) % E, np.arange(P) // E
    same = e[:, None] == e[None, :]
    t["same"] = same.astype(np.float32)
    t["before"] = (same & (t8[:, None] < t8[None, :])).astype(np.float32)
    t["bits"] = np.broadcast_to(np.array([-1] + [1 << (31 - i) for i in range(1, 32)] + [0], np.int32), (P, 33))
    t["base"] = (e * CAP - 1 - E * CAP).astype(np.float32).reshape(P, 1)
    kj = np.arange(KEYS2)[None, :] - PM
    t["mask"] = np.where((kj < 0) | (np.arange(P)[:, None] >= kj), 0.0, NEG).astype(np.float32).reshape(P, 1, KEYS2)
    return {k: np.ascontiguousarray(a) for k, a in t.items()}


OUT = ((B * S, D), "float32")


def declare(nc, arrays):
    io = {k: nc.dram_tensor(f"in_{k}", a.shape, mybir.dt.from_np(a.dtype), kind="ExternalInput").ap()
          for k, a in arrays.items()}
    io["out"] = nc.dram_tensor("out_0", OUT[0], F32, kind="ExternalOutput").ap()
    return io


def kernel(**inputs):
    import concourse.bacc as bacc
    from concourse.bass_utils import run_bass_kernel_spmd as run
    nc = bacc.Bacc("TRN2", target_bir_lowering=False, num_devices=1)
    arrays = layout(inputs)
    build(nc, declare(nc, arrays))
    r = run(nc, [{f"in_{k}": a for k, a in arrays.items()}], core_ids=[0])
    return r.results[0]["out_0"].reshape(B, S, D)
```

```python
import concourse.bass as bass
from concourse import mybir
from contextlib import ExitStack
import numpy as np

F32 = mybir.dt.float32
I32 = mybir.dt.int32
U32 = mybir.dt.uint32
ALU = mybir.AluOpType
ACT = mybir.ActivationFunctionType
AX = mybir.AxisListType

P = 128
B, S, D = 8, 256, 256
NT = S // P
KD = D // P
PAIRS = B // 2
L, H, DK, F, V = 4, 16, 16, 1024, 7500
FT = F // P
STRIP = 64 // DK
TOK_EPS = 1e-6
HEADS2, DH2, PM = 16, 64, 16
INNER = HEADS2 * DH2
CT = INNER // P
KEYS2 = PM + P
LN_EPS, RMS_EPS = 1e-5, 1e-6
E, TOPK, HID, SHARED = 16, 2, 512, 2
N = B * S
CAP = -(-(N * TOPK * 5) // (E * 4))
HT = HID // P
NEG = float(np.finfo(np.float32).min)

C_LNA, C_LNB, C_BQ, C_BK, C_B1, COLS = 0, 4, 8, 10, 12, 20
R_BV, R_BO, R_B2 = 0, 1, 2


class Tally:

    def __init__(self, sem, per, credit=0):
        self.sem, self.per, self.credit = sem, per, credit
        self.base, self.n = 0, 0

    def turn(self, t):
        self.base, self.n = t * self.per, 0

    def up(self, ins, by=1):
        ins.then_inc(self.sem, by)
        self.n += by

    def wait(self, eng, n=None, t=None):
        base = self.base if t is None else t * self.per
        eng.wait_ge(self.sem, base + self.credit + (self.n if n is None else n))

    def whole(self):
        assert self.n == self.per, (self.sem, self.n, self.per)


def embed_and_encoder(nc, io, h, wqkv, wout, s_w2):
    ctx = ExitStack()
    with ctx:
        sb = lambda name, shape, dt=F32: ctx.enter_context(nc.sbuf_tensor(name, shape, dt))
        pb = lambda name, shape: ctx.enter_context(nc.psum_tensor(name, shape, F32))
        sem = lambda name: ctx.enter_context(nc.semaphore(name))

        weights = [sb(f"weights{i}", [P, 6144]) for i in range(2)]
        cols = [sb(f"cols{i}", [P, COLS]) for i in range(2)]
        rows = [sb(f"rows{i}", [P, 3, D]) for i in range(2)]
        wqkvo = [w[:, 0:2048].rearrange("p (t k n) -> p t k n", t=4, k=KD) for w in weights]
        w1 = [w[:, 2048:4096].rearrange("p (k n) -> p k n", k=KD) for w in weights]
        w2 = [w[:, 4096:6144].rearrange("p (k n) -> p k n", k=FT) for w in weights]
        ident = sb("ident", [P, P])
        qmask = sb("qmask", [P, STRIP])
        half = sb("half", [P, NT])
        idx = sb("idx", [P, B * NT], I32)
        idxf = sb("idxf", [P, B * NT])
        idxn = sb("idxn", [P, B * NT])
        idxu = sb("idxu", [P, B * NT], U32)
        pe_sb = sb("pe_sb", [P, NT, D])
        stats = [sb(f"stats{a}", [P, NT, 6]) for a in range(2)]
        mv = [sb(f"mv{a}", [P, NT, 2]) for a in range(2)]
        sd = [sb(f"sd{a}", [P, NT]) for a in range(2)]
        den = [sb(f"den{a}", [P, NT]) for a in range(2)]
        rstd = [sb(f"rstd{a}", [P, NT]) for a in range(2)]
        yn1 = [sb(f"yn1_{a}", [P, NT, D]) for a in range(2)]
        yn2 = [sb(f"yn2_{a}", [P, NT, D]) for a in range(2)]
        yT = [sb(f"yT{a}", [P, KD, S]) for a in range(2)]
        qm = [sb(f"qm{a}", [P, STRIP, KD, S]) for a in range(2)]
        kT = [sb(f"kT{a}", [P, KD, S]) for a in range(2)]
        v = [sb(f"v{a}", [P, NT, H // 2, 2, 2 * DK]) for a in range(2)]
        nmax = [sb(f"nmax{a}", [P, NT * H]) for a in range(2)]
        rsum = [sb(f"rsum{a}", [P, NT * H]) for a in range(2)]
        rinv = [sb(f"rinv{a}", [P, NT * H]) for a in range(2)]
        probs = [sb(f"probs{i}", [P, 2, S]) for i in range(8)]
        pts = [sb(f"pts{i}", [P, 2, NT, P]) for i in range(4)]
        rb = [sb(f"rb{a}", [P, NT, H, DK]) for a in range(2)]
        rT = [sb(f"rT{a}", [P, KD, S]) for a in range(2)]
        oT = [sb(f"oT{a}", [P, KD, S]) for a in range(2)]
        aT = [sb(f"aT{a}", [P, FT, S]) for a in range(2)]
        scratch = sb("scratch", [P, 9])

        bank = [pb(f"bank{i}", [P, 512]) for i in range(8)]

        order, ring = [], [0]

        def use(u, b=None):
            if b is None:
                b = ring[0] % 4
                ring[0] += 1
            order.append((u, b))

        def use_group(g):
            for j in range(4):
                use((g // 4, "S", 4 * (g % 4) + j))

        use((0, "yT", 0), 5)
        use((1, "yT", 0), 6)
        for n, b in ("q", None), ("k", None), ("v", 4):
            use((0, n, 0), b)
        use_group(0)
        for n, b in ("q", 5), ("k", 6), ("v", 7):
            use((1, n, 0), b)
        for g in range(1, 9):
            if g < 8:
                use_group(g)
            if g == 5:
                use((0, "rT", 0))
            if g == 6:
                use((0, "wo", 0), 6)
            for j in range(4):
                u = 4 * (g - 1) + j
                use((u // 16, "pt", u % 16), 4 + u % 2)
                if u in (2, 18):
                    use((u // 16, "o", 0), 6 + u // 16)
            if g == 7:
                use((0, "y2T", 0), 6)
        use((0, "w1", 0), 6)
        use((1, "rT", 0))
        for i in range(1, 4):
            use((0, "w1", i))
        use((1, "wo", 0))
        use((0, "w2", 0), 4)
        use((1, "y2T", 0), 7)
        for i in range(4):
            use((1, "w1", i))
        use((1, "w2", 0), 7)
        place = {u: (b, sum(c == b for _, c in order[:n])) for n, (u, b) in enumerate(order)}
        USES = [sum(c == b for _, c in order) for b in range(8)]

        s_const = sem("s_const")
        s_idx = sem("s_idx")
        s_gather = [sem(f"s_gather{s}") for s in range(B)]
        s_h = sem("s_h")
        s_w = [sem(f"s_w{i}") for i in range(2)]
        s_wf = [sem(f"s_wf{i}") for i in range(2)]
        s_full = [sem(f"s_full{i}") for i in range(8)]
        s_free = [sem(f"s_free{i}") for i in range(8)]
        NLOAD = 3
        FIRST = 4 + 2 + 2 + 2 * 5
        names = dict(yn1_ready=2, yn2_ready=2, max_ready=32, rb_ready=2,
                     var1_ready=2, var2_ready=2, sd1_ready=2, sd2_ready=2, dve_step=26)
        sems = {n: sem(n) for n in names}

        def tallies():
            return {n: Tally(sems[n], per) for n, per in names.items()}

        def acquire(pe, t, u):
            b, use = place[u]
            pe.wait_ge(s_free[b], t * USES[b] + use + 1)
            return bank[b]

        def filled(ins, u):
            ins.then_inc(s_full[place[u][0]], 1)

        def take(eng, t, u):
            b, use = place[u]
            eng.wait_ge(s_full[b], t * USES[b] + use + 1)
            return bank[b]

        def release(ins, u):
            ins.then_inc(s_free[place[u][0]], 1)

        def evacuated(eng, t, u):
            b, use = place[u]
            eng.wait_ge(s_free[b], t * USES[b] + use + 2)

        def turns(eng):
            with eng.Fori(0, L // 2) as l2:
                for lp in range(2):
                    with eng.Fori(0, PAIRS) as p:
                        yield l2, lp, p, l2 * (2 * PAIRS) + (lp * PAIRS) + p

        block = ctx.enter_context(nc.Block())

        @block.sync
        def _(sp):
            sp.dma_start(idx[:], io["idx"]).then_inc(s_idx, 16)
            sp.dma_start(pe_sb[:], io["pe"]).then_inc(s_const, 16)
            sp.dma_start(ident[:], io["ident"]).then_inc(s_const, 16)
            sp.dma_start(qmask[:], io["qmask"]).then_inc(s_const, 16)
            for l in range(L):
                if l >= 2:
                    sp.wait_ge(sems["dve_step"], FIRST + names["dve_step"] * (l - 1) * PAIRS)
                sp.dma_start(weights[l % 2][:, 0:2048], io["wtok"][l, :, 0:2048]).then_inc(s_w[l % 2], 16)
                sp.dma_start(cols[l % 2][:], io["cols"][l]).then_inc(s_w[l % 2], 16)
                sp.dma_start(rows[l % 2][:], io["rows"][l].partition_broadcast(P)).then_inc(s_w[l % 2], 16)
                if l == 0:
                    for s in range(2):
                        sp.wait_ge(s_gather[s], 16 * NT)
                sp.dma_start(weights[l % 2][:, 2048:], io["wtok"][l, :, 2048:]).then_inc(s_wf[l % 2], 16)
            sp.dma_start(wqkv[:], io["wqkv"]).then_inc(s_w2, 16)
            sp.dma_start(wout[:], io["wout"]).then_inc(s_w2, 16)

        @block.gpsimd
        def _(pool):
            nc.gpsimd.memset(half[:], 0.5).then_inc(sems["sd1_ready"], 1)
            pool.wait_ge(s_idx, 17)
            def gather(tiles):
                for j in tiles:
                    pool.indirect_dma_start(h[:, j // NT, j % NT, :], None, io["emb"],
                                            bass.IndirectOffsetOnAxis(ap=idxu[:, j:j + 1], axis=0)).then_inc(s_gather[j // NT], 16)

            gather(range(B))
            pool.wait_ge(sems["sd1_ready"], 1)
            pool.wait_ge(s_const, 48)

            def root(T, k, a, t):
                T[f"var{k}_ready"].wait(pool, a + 1, t)
                nc.gpsimd.tensor_tensor(sd[a][:], mv[a][:, :, 1], half[:], ALU.pow).then_inc(sems[f"sd{k}_ready"], 1)

            for a in range(2):
                root(tallies(), 1, a, 0)
            gather(range(B, B * NT))
            for s in range(2, B):
                pool.wait_ge(s_gather[s], 16 * NT)
                nc.gpsimd.tensor_tensor(h[:, s], h[:, s], pe_sb[:], ALU.add).then_inc(s_h, 1)
            for l2, lp, p, t in turns(pool):
                for k, turn in ((1, t + 1), (2, t)):
                    for a in range(2):
                        root(tallies(), k, a, turn)

        @block.tensor
        def _(pe):
            pe.wait_ge(s_const, 48)

            def transposed(t, u, src, T, ready, n):
                g = acquire(pe, t, u)
                T[ready].wait(pe, n, t)
                for k in range(KD):
                    for i in range(NT):
                        last = pe.transpose(g[:, k * S + i * P:k * S + i * P + P],
                                            src[:, i, k * P:(k + 1) * P], ident[:])
                filled(last, u)

            for a in range(2):
                transposed(0, (a, "yT", 0), yn1[a], tallies(), "yn1_ready", a + 1)
            for l2, lp, p, t in turns(pe):
                T = tallies()
                for x in T.values():
                    x.turn(t)
                wq, wk, wv, wo = (wqkvo[lp][:, i] for i in range(4))

                def feature_major(a, name, w):
                    g = acquire(pe, t, (a, name, 0))
                    for m in range(KD):
                        for k in range(KD):
                            last = pe.matmul(g[:, m * S:(m + 1) * S], w[:, k, m * P:(m + 1) * P],
                                             yT[a][:, k, :], start=(k == 0), stop=(k == KD - 1))
                    filled(last, (a, name, 0))

                def token_major(a, name, src, w, kt):
                    g = acquire(pe, t, (a, name, 0))
                    for i in range(NT):
                        for k in range(kt):
                            last = pe.matmul(g[:, i * D:(i + 1) * D], src[:, k, i * P:(i + 1) * P],
                                             w[:, k, :], start=(k == 0), stop=(k == kt - 1))
                    filled(last, (a, name, 0))

                def scores(grp):
                    a = grp // 4
                    if grp % 4 == 0:
                        evacuated(pe, t, (a, "q", 0))
                        evacuated(pe, t, (a, "k", 0))
                    qt, c = (grp % 4) // 2, grp % 2
                    units = [(a, "S", 4 * (grp % 4) + j) for j in range(4)]
                    gs = []
                    for odd in range(2):
                        for j in range(4):
                            if not odd:
                                gs.append(acquire(pe, t, units[j]))
                            r = slice(64 * (j // 2), 64 * (j // 2) + 64)
                            last = pe.matmul(gs[j][:, odd * S:(odd + 1) * S],
                                             qm[a][r, 2 * (j % 2) + odd, c, qt * P:(qt + 1) * P], kT[a][r, c, :],
                                             start=True, stop=True)
                            if odd:
                                filled(last, units[j])

                def turn_probs(u):
                    a, i = divmod(u, 16)
                    g = acquire(pe, t, (a, "pt", i))
                    evacuated(pe, t, (a, "S", i))
                    for x in range(2):
                        for kb in range(NT):
                            last = pe.transpose(g[:, (NT * x + kb) * P:(NT * x + kb + 1) * P], probs[u % 8][:, x, kb * P:(kb + 1) * P], ident[:])
                    filled(last, (a, "pt", i))

                def pv(u):
                    a, i = divmod(u, 16)
                    if i == 0:
                        acquire(pe, t, (a, "o", 0))
                    if u >= 30:
                        evacuated(pe, t, (a, "pt", i))
                    qt, c, j = i // 8, (i // 4) % 2, i % 4
                    out = bank[6 + a][32 * j:32 * j + 32, c * S + qt * P:c * S + (qt + 1) * P]
                    for x in range(2):
                        for kb in range(NT):
                            last = pe.matmul(out, v[a][:, kb, 4 * c + j, x, :], pts[u % 4][:, x, kb, :],
                                             start=(x == 0 and kb == 0), stop=(x == 1 and kb == NT - 1))
                    if i == 15:
                        filled(last, (a, "o", 0))

                def ffn_up(a, i):
                    evacuated(pe, t, (a, "y2T", 0))
                    g = acquire(pe, t, (a, "w1", i))
                    for m in range(2):
                        f = 2 * i + m
                        for k in range(KD):
                            last = pe.matmul(g[:, m * S:(m + 1) * S], w1[lp][:, k, f * P:(f + 1) * P],
                                             yT[a][:, k, :], start=(k == 0), stop=(k == KD - 1))
                    filled(last, (a, "w1", i))

                def ffn_down(a):
                    g = acquire(pe, t, (a, "w2", 0))
                    for i in range(NT):
                        for f in range(FT):
                            if i == 0 and f % 2 == 0:
                                evacuated(pe, t, (a, "w1", f // 2))
                            last = pe.matmul(g[:, i * D:(i + 1) * D], aT[a][:, f, i * P:(i + 1) * P],
                                             w2[lp][:, f, :], start=(f == 0), stop=(f == FT - 1))
                    filled(last, (a, "w2", 0))

                def qkv(a):
                    evacuated(pe, t, (a, "yT", 0))
                    feature_major(a, "q", wq)
                    feature_major(a, "k", wk)
                    token_major(a, "v", yT[a], wv, KD)

                def r_T(a):
                    transposed(t, (a, "rT", 0), rb[a][:].rearrange("p i n d -> p i (n d)"), T, "rb_ready", a + 1)

                def project_out(a):
                    evacuated(pe, t, (a, "o", 0))
                    token_major(a, "wo", oT[a], wo, KD)

                pe.wait_ge(s_w[lp], l2 * (16 * NLOAD) + 16 * NLOAD)
                qkv(0)
                scores(0)
                qkv(1)
                for grp in range(1, 9):
                    if grp < 8:
                        scores(grp)
                    if grp == 5:
                        r_T(0)
                    if grp == 6:
                        project_out(0)
                    for j in range(4):
                        u = 4 * (grp - 1) + j
                        turn_probs(u)
                        if u >= 2:
                            pv(u - 2)
                    if grp == 7:
                        transposed(t, (0, "y2T", 0), yn2[0], T, "yn2_ready", 1)
                pv(30)
                pv(31)
                pe.wait_ge(s_wf[lp], l2 * 16 + 16)
                ffn_up(0, 0)
                r_T(1)
                for i in range(1, 4):
                    ffn_up(0, i)
                project_out(1)
                ffn_down(0)
                transposed(t, (1, "y2T", 0), yn2[1], T, "yn2_ready", 2)
                for a in range(2):
                    transposed(t + 1, (a, "yT", 0), yn1[a], T, "yn1_ready", a + 1)
                for i in range(4):
                    ffn_up(1, i)
                ffn_down(1)

        @block.scalar
        def _(act):
            for l2, lp, p, t in turns(act):
                T = tallies()
                for x in T.values():
                    x.turn(t)

                def y_out(a, name, ln):
                    u = (a, name, 0)
                    g = take(act, t, u)
                    for k in range(KD):
                        last = nc.scalar.activation(yT[a][:, k, :], g[:, k * S:(k + 1) * S], ACT.Identity,
                                                    scale=cols[lp][:, C_LNA + 2 * ln + k:C_LNA + 2 * ln + k + 1],
                                                    bias=cols[lp][:, C_LNB + 2 * ln + k:C_LNB + 2 * ln + k + 1])
                    release(last, u)

                def exps(u):
                    a, i = divmod(u, 16)
                    un = (a, "S", i)
                    T["max_ready"].wait(act, u + 1)
                    g = bank[place[un][0]]
                    qt, c, j = i // 8, (i // 4) % 2, i % 4
                    for x in range(2):
                        col = qt * H + 8 * c + 2 * j + x
                        last = nc.scalar.activation(probs[u % 8][:, x, :], g[:, x * S:(x + 1) * S], ACT.Exp,
                                                    bias=nmax[a][:, col:col + 1], accum_out=rsum[a][:, col:col + 1])
                    release(last, un)

                def copy_pt(u):
                    un = (u // 16, "pt", u % 16)
                    g = take(act, t, un)
                    release(nc.scalar.activation(pts[u % 4][:], g[:].rearrange("p (x k s) -> p x k s", x=2, k=NT), ACT.Copy), un)

                def r_out(a):
                    u = (a, "rT", 0)
                    g = take(act, t, u)
                    release(nc.scalar.activation(rT[a][:], g[:], ACT.Copy), u)

                def relu(a, i):
                    u = (a, "w1", i)
                    g = take(act, t, u)
                    for m in range(2):
                        f = 2 * i + m
                        last = nc.scalar.activation(aT[a][:, f, :], g[:, m * S:(m + 1) * S], ACT.Relu,
                                                    bias=cols[lp][:, C_B1 + f:C_B1 + f + 1])
                    release(last, u)

                def k_out(a):
                    u = (a, "k", 0)
                    g = take(act, t, u)
                    for m in range(KD):
                        last = nc.scalar.activation(kT[a][:, m, :], g[:, m * S:(m + 1) * S], ACT.Identity,
                                                    bias=cols[lp][:, C_BK + m:C_BK + m + 1])
                    release(last, u)

                act.wait_ge(s_w[lp], l2 * (16 * NLOAD) + 16 * NLOAD)
                y_out(0, "yT", 0)
                y_out(1, "yT", 0)
                k_out(0)
                for j in range(4):
                    exps(j)
                k_out(1)
                for grp in range(1, 9):
                    for j in range(4):
                        if grp < 8:
                            exps(4 * grp + j)
                        if grp == 5 and j == 0:
                            r_out(0)
                        if j % 2:
                            copy_pt(4 * (grp - 1) + j)
                        if grp == 8 and j == 1:
                            y_out(0, "y2T", 1)
                r_out(1)
                relu(0, 1)
                relu(0, 3)
                y_out(1, "y2T", 1)
                relu(1, 1)
                relu(1, 3)

        @block.vector
        def _(dve):
            for i in range(8):
                nc.vector.memset(scratch[:, i:i + 1], 0.0).then_inc(s_free[i], 1)
            dve.wait_ge(s_idx, 16)
            step = sems["dve_step"]
            nc.vector.tensor_copy(idxf[:], idx[:]).then_inc(step, 1)
            dve.wait_ge(step, 1)
            nc.vector.tensor_scalar(idxn[:], idxf[:], 0.0, float(V), ALU.is_lt, ALU.mult).then_inc(step, 1)
            dve.wait_ge(step, 2)
            nc.vector.tensor_tensor(idxf[:], idxf[:], idxn[:], ALU.add).then_inc(step, 1)
            dve.wait_ge(step, 3)
            nc.vector.tensor_scalar(idxn[:], idxf[:], 0.0, float(V - 1), ALU.max, ALU.min).then_inc(step, 1)
            dve.wait_ge(step, 4)
            nc.vector.tensor_copy(idxu[:], idxn[:]).then_inc(s_idx, 1)
            dve.wait_ge(s_const, 48)
            for a in range(2):
                nc.vector.memset(v[a][:], 0.0).then_inc(step, 1)
            start = Tally(step, 0)
            start.n = 6

            def positions(s):
                dve.wait_ge(s_gather[s], 16 * NT)
                start.up(nc.vector.tensor_tensor(h[:, s], h[:, s], pe_sb[:], ALU.add))

            for s in range(2):
                positions(s)

            def after_held(chain):
                chain.wait(dve)
                chain.up(nc.vector.memset(scratch[:, 8:], 0.0))

            def stats_of(chain, k, a, seq):
                after_held(chain)
                for i in range(NT):
                    last = nc.vector.bn_stats(stats[a][:, i, :], h[:, seq, i, :])
                chain.up(last)
                after_held(chain)
                for i in range(NT):
                    last = nc.vector.bn_aggr(mv[a][:, i, :], stats[a][:, i, :])
                last.then_inc(sems[f"var{k}_ready"], 1)

            def normalise(chain, T, k, a, seq, t):
                T[f"sd{k}_ready"].credit = 2 - k
                T[f"sd{k}_ready"].wait(dve, a + 1, t)
                chain.up(nc.vector.tensor_scalar(den[a][:], sd[a][:], float((D / (D - 1)) ** 0.5), TOK_EPS, ALU.mult, ALU.add))
                chain.wait(dve)
                chain.up(nc.vector.reciprocal(rstd[a][:], den[a][:]))
                chain.wait(dve)
                for i in range(NT):
                    last = nc.vector.tensor_scalar((yn1, yn2)[k - 1][a][:, i, :], h[:, seq, i, :], mv[a][:, i, 0:1],
                                                   rstd[a][:, i:i + 1], ALU.subtract, ALU.mult)
                last.then_inc(sems[f"yn{k}_ready"], 1)

            for a in range(2):
                stats_of(start, 1, a, a)
            for a in range(2):
                normalise(start, tallies(), 1, a, a, 0)
            assert start.n == FIRST
            for l2, lp, p, t in turns(dve):
                T = tallies()
                for x in T.values():
                    x.turn(t)
                T["dve_step"].credit = FIRST
                chain = T["dve_step"]
                ahead = lambda a: ((p + 1) & (PAIRS - 1)) * 2 + a

                def q_out(a):
                    u = (a, "q", 0)
                    g = take(dve, t, u)
                    for x in range(STRIP):
                        for m in range(KD):
                            last = nc.vector.tensor_scalar(qm[a][:, x, m, :], g[:, m * S:(m + 1) * S],
                                                           cols[lp][:, C_BQ + m:C_BQ + m + 1], qmask[:, x:x + 1],
                                                           ALU.add, ALU.mult)
                    release(last, u)

                def v_out(a):
                    u = (a, "v", 0)
                    g = take(dve, t, u)
                    gv = g[:].rearrange("p (i n x d) -> p i n x d", i=NT, x=2, d=DK)
                    bv = rows[lp][:, R_BV, :].rearrange("p (n x d) -> p n x d", x=2, d=DK)
                    for i in range(NT):
                        for x in range(2):
                            last = nc.vector.tensor_tensor(v[a][:, i, :, x, x * DK:(x + 1) * DK], gv[:, i, :, x, :],
                                                           bv[:, :, x, :], ALU.add)
                    release(last, u)

                def row_max(u):
                    a, i = divmod(u, 16)
                    g = take(dve, t, (a, "S", i))
                    qt, c, j = i // 8, (i // 4) % 2, i % 4
                    col = qt * H + 8 * c + 2 * j
                    nc.vector.tensor_reduce(nmax[a][:, col:col + 2], g[:].rearrange("p (x s) -> p x s", x=2),
                                            AX.X, ALU.max, negate=True).then_inc(sems["max_ready"], 1)

                def copy_pt(u):
                    un = (u // 16, "pt", u % 16)
                    g = take(dve, t, un)
                    release(nc.vector.tensor_copy(pts[u % 4][:], g[:].rearrange("p (x k s) -> p x k s", x=2, k=NT)), un)

                def recips(a):
                    evacuated(dve, t, (a, "S", 15))
                    chain.up(nc.vector.reciprocal(rinv[a][:], rsum[a][:]))
                    chain.wait(dve)
                    nc.vector.tensor_copy(rb[a][:], rinv[a][:].rearrange("p (i n x) -> p i n x", i=NT, x=1)
                                          .to_broadcast((P, NT, H, DK))).then_inc(sems["rb_ready"], 1)

                def o_norm(a):
                    evacuated(dve, t, (a, "rT", 0))
                    g = take(dve, t, (a, "o", 0))
                    release(nc.vector.tensor_tensor(oT[a][:].rearrange("p k s -> p (k s)"), g[:],
                                                    rT[a][:].rearrange("p k s -> p (k s)"), ALU.mult), (a, "o", 0))

                def residual(a, name, row):
                    u = (a, name, 0)
                    g = take(dve, t, u)
                    ins = nc.vector.tensor_tensor(h[:, 2 * p + a], h[:, 2 * p + a], g[:].rearrange("p (i d) -> p i d", i=NT), ALU.add)
                    release(ins, u)
                    evacuated(dve, t, u)
                    return nc.vector.tensor_tensor(h[:, 2 * p + a], h[:, 2 * p + a],
                                                   rows[lp][:, row:row + 1, :].to_broadcast((P, NT, D)), ALU.add)

                def relu(a, i):
                    u = (a, "w1", i)
                    g = take(dve, t, u)
                    for m in range(2):
                        f = 2 * i + m
                        last = nc.vector.tensor_scalar(aT[a][:, f, :], g[:, m * S:(m + 1) * S],
                                                       cols[lp][:, C_B1 + f:C_B1 + f + 1], 0.0, ALU.add, ALU.max)
                    release(last, u)

                def residual_add(a, name, row):
                    chain.up(residual(a, name, row))

                dve.wait_ge(s_w[lp], l2 * (16 * NLOAD) + 16 * NLOAD)
                q_out(0)
                v_out(0)
                for j in range(4):
                    row_max(j)
                q_out(1)
                v_out(1)
                for grp in range(1, 9):
                    for j in range(4):
                        if grp < 8:
                            row_max(4 * grp + j)
                        if j % 2:
                            copy_pt(4 * (grp - 1) + j - 1)
                        if grp == 6 and j == 1:
                            residual_add(0, "wo", R_BO)
                        if grp == 7 and j == 1:
                            normalise(chain, T, 2, 0, 2 * p, t)
                    if grp == 1:
                        dve.wait_ge(s_h, B - 2)
                    if grp in (1, 2):
                        stats_of(chain, 1, grp - 1, ahead(grp - 1))
                    if grp in (2, 3):
                        normalise(chain, T, 1, grp - 2, ahead(grp - 2), t + 1)
                    if grp == 4:
                        recips(0)
                    if grp == 5:
                        o_norm(0)
                    if grp == 6:
                        stats_of(chain, 2, 0, 2 * p)
                recips(1)
                relu(0, 0)
                o_norm(1)
                relu(0, 2)
                residual_add(1, "wo", R_BO)
                stats_of(chain, 2, 1, 2 * p + 1)
                normalise(chain, T, 2, 1, 2 * p + 1, t)
                residual_add(0, "w2", R_B2)
                relu(1, 0)
                relu(1, 2)
                residual_add(1, "w2", R_B2)
                chain.whole()


def windowed_attention(nc, io, h, wqkv, wout, s_w2):
    ctx = ExitStack()
    with ctx:
        sb = lambda name, shape, dt=F32: ctx.enter_context(nc.sbuf_tensor(name, shape, dt))
        pb = lambda name, shape: ctx.enter_context(nc.psum_tensor(name, shape, F32))
        sem = lambda name: ctx.enter_context(nc.semaphore(name))

        ident = sb("w_ident", [P, P])
        mask = sb("mask", [P, 1, KEYS2])
        normab = sb("normab", [P, 2, D])
        gamma = sb("gamma", [P, KD])
        pmk = sb("pmk", [P, CT, 1, PM])
        pmv = sb("pmv", [PM, INNER])
        expo = sb("expo", [P, 2, NT])
        stats = [sb(f"w_stats{a}", [P, NT, 6]) for a in range(2)]
        mv = [sb(f"w_mv{a}", [P, NT, 2]) for a in range(2)]
        mv2 = [sb(f"w_mv2{a}", [P, NT, 2]) for a in range(2)]
        sd = [sb(f"w_sd{a}", [P, NT]) for a in range(2)]
        sd2 = [sb(f"w_sd2{a}", [P, NT]) for a in range(2)]
        den = [sb(f"w_den{a}", [P, NT]) for a in range(2)]
        rstd = [sb(f"w_rstd{a}", [P, NT]) for a in range(2)]
        yn = [sb(f"w_yn{a}", [P, NT, D]) for a in range(2)]
        yT = [sb(f"w_yT{a}", [P, KD, S]) for a in range(2)]
        qT = [sb(f"w_qT{a}", [P, CT, S]) for a in range(2)]
        kT = [sb(f"w_kT{a}", [P, CT, NT, KEYS2]) for a in range(2)]
        v = [sb(f"w_v{a}", [P, NT, INNER]) for a in range(2)]
        nmax = [sb(f"w_nmax{a}", [P, NT * HEADS2]) for a in range(2)]
        rsum = [sb(f"w_rsum{a}", [P, NT * HEADS2]) for a in range(2)]
        rinv = [sb(f"w_rinv{a}", [P, NT * HEADS2]) for a in range(2)]
        probs = [sb(f"w_probs{i}", [P, 2, KEYS2]) for i in range(8)]
        pts = [sb(f"w_pts{i}", [P, 2, 2, P]) for i in range(4)]
        rb = [sb(f"w_rb{i}", [P, 8, DH2]) for i in range(2)]
        rT = [sb(f"w_rT{i}", [P, 4, P]) for i in range(2)]
        oT = [sb(f"w_oT{a}", [P, CT, S]) for a in range(2)]
        scratch = sb("w_scratch", [P, 17])
        bank = [pb(f"w_bank{i}", [P, 512]) for i in range(8)]

        NEXT = 1
        second = [(1, n, i, 0) for n in "qkv" for i in range(4)]
        first = [(0, n, i, NEXT) for n in "qkv" for i in range(4)]
        between = {(0, 3): second[:3]}
        for g in range(1, 4):
            for x, j in enumerate((0, 2, 3)):
                between[g, j] = [second[3 * g + x]]
        between[4, 0] = [(0, "yT", 0, NEXT)]
        between[4, 3] = [first[0]]
        between[5, 0], between[5, 1], between[5, 3] = [first[1]], [first[2]], [first[3]]
        between[6, 0], between[6, 1], between[6, 3] = [first[4]], [(0, "wo", 0, 0)], [first[5]]
        between[7, 0], between[7, 1], between[7, 3] = [first[6]], [first[7]], [first[8], (1, "yT", 0, NEXT)]
        between[8, 1] = [first[9]]
        tail = first[10:]

        order, ring = [], [0]

        def use(u, b=None):
            if b is None:
                b = ring[0] % 4
                ring[0] += 1
            order.append((u, b))

        for g in range(9):
            if g < 8:
                for j in range(4):
                    use((g // 4, "S", 4 * (g % 4) + j))
            for j in range(4):
                if g >= 1:
                    u = 4 * (g - 1) + j
                    use((u // 16, "pt", u % 16), 4 + u % 2)
                    if u % 4 == 2:
                        use((u // 16, "o", (u % 16) // 4), 6 + (u // 4) % 2)
                if g >= 2 and j == 1:
                    use(((g - 2) // 4, "rT", (g - 2) % 4))
                for n, (*u, _) in enumerate(between.get((g, j), ())):
                    use(tuple(u), 4 + n if g == 0 else None)
        use((1, "rT", 3))
        for *u, _ in tail:
            use(tuple(u))
        use((1, "wo", 0))
        ahead_units = [tuple(u[:3]) for key in sorted(between) for u in between[key] if u[3]]
        ahead_units += [tuple(u[:3]) for u in tail]
        place = {u: (b, sum(c == b for _, c in order[:n])) for n, (u, b) in enumerate(order)}
        USES = [sum(c == b for _, c in order) for b in range(8)]
        made = lambda part, u: part == "turn" or (u in ahead_units) == (part == "before")
        made_on = {(part, b): [place[u][1] for u, c in order if c == b and made(part, u)] + [USES[b]]
                   for part in ("before", "turn", "last") for b in range(8)}
        assert not any(made_on["last", b][0] for b in range(8))
        part = ["before"]

        def base(u, t):
            return (t if u in ahead_units else t + 1) * USES[place[u][0]]

        def signals(u):
            b, use = place[u]
            uses = made_on[part[0], b]
            return uses[uses.index(use) + 1] - use

        s_const = sem("w_const")
        s_full = [sem(f"w_full{i}") for i in range(8)]
        s_free = [sem(f"w_free{i}") for i in range(8)]
        NORM = 2 * 13
        names = dict(yn_ready=2, max_ready=32, rb_ready=8, var_ready=4, sd_ready=4, dve_step=40 + NORM)
        sems = {n: sem("w_" + n) for n in names}
        FIRST = 1 + NORM
        NCONST = 6

        def tallies(t):
            T = {n: Tally(sems[n], per) for n, per in names.items()}
            for x in T.values():
                x.turn(t)
            return T

        def acquire(pe, t, u):
            b, use = place[u]
            pe.wait_ge(s_free[b], base(u, t) + use + 1)
            return bank[b]

        def filled(ins, u):
            ins.then_inc(s_full[place[u][0]], signals(u))

        def take(eng, t, u):
            b, use = place[u]
            eng.wait_ge(s_full[b], base(u, t) + use + 1)
            return bank[b]

        def release(ins, u):
            ins.then_inc(s_free[place[u][0]], signals(u))

        def evacuated(eng, t, u):
            b, use = place[u]
            eng.wait_ge(s_free[b], base(u, t) + use + 2)

        def turns(eng):
            with eng.Fori(0, PAIRS - 1) as t:
                part[0] = "turn"
                yield t, False
            part[0] = "last"
            yield PAIRS - 1, True
            part[0] = "before"

        block = ctx.enter_context(nc.Block())

        @block.sync
        def _(sp):
            for dst, src in ((ident[:], io["ident"]), (mask[:], io["mask"]), (normab[:], io["normab"].partition_broadcast(P)),
                             (gamma[:], io["gamma"]), (pmk[:], io["pmk"]), (pmv[:], io["pmv"])):
                sp.dma_start(dst, src).then_inc(s_const, 16)

        @block.gpsimd
        def _(pool):
            nc.gpsimd.memset(expo[:, 0, :], 0.5).then_inc(sems["sd_ready"], 1)
            nc.gpsimd.memset(expo[:, 1, :], -0.5).then_inc(sems["sd_ready"], 1)
            pool.wait_ge(sems["sd_ready"], 2)
            with pool.Fori(0, PAIRS) as t:
                T = tallies(t)
                for k in range(4):
                    a, second = divmod(k, 2)
                    T["var_ready"].wait(pool, k + 1)
                    if not second:
                        ins = nc.gpsimd.tensor_tensor(sd[a][:], mv[a][:, :, 1], expo[:, 0, :], ALU.pow)
                    else:
                        ins = nc.gpsimd.tensor_tensor(sd2[a][:], den[a][:], expo[:, 1, :], ALU.pow)
                    ins.then_inc(sems["sd_ready"], 1)

        @block.tensor
        def _(pe):
            pe.wait_ge(s_const, 16 * NCONST)
            pe.wait_ge(s_w2, 32)

            def project(u, t):
                a, n, i = u
                if n == "wo":
                    return project_out(a, t)
                if n == "yT":
                    g = acquire(pe, t, u)
                    tallies(t)["yn_ready"].wait(pe, 1 + a)
                    for k in range(KD):
                        for i in range(NT):
                            last = pe.transpose(g[:, k * S + i * P:k * S + i * P + P],
                                                yn[a][:, i, k * P:(k + 1) * P], ident[:])
                    return filled(last, u)
                if n == "q" and i == 0:
                    evacuated(pe, t, (a, "yT", 0))
                g = acquire(pe, t, u)
                if n in "qk":
                    for x in range(2):
                        m = "qk".index(n) * CT + 2 * i + x
                        for k in range(KD):
                            last = pe.matmul(g[:, x * S:(x + 1) * S], wqkv[:, k, m * P:(m + 1) * P],
                                             yT[a][:, k, :], start=(k == 0), stop=(k == KD - 1))
                else:
                    w, half = divmod(i, 2)
                    for k in range(KD):
                        last = pe.matmul(g[:], yT[a][:, k, w * P:(w + 1) * P],
                                         wqkv[:, k, 2 * INNER + half * 512:2 * INNER + (half + 1) * 512],
                                         start=(k == 0), stop=(k == KD - 1))
                filled(last, u)

            def project_out(a, t):
                u = (a, "wo", 0)
                g = acquire(pe, t, u)
                evacuated(pe, t, (a, "o", 2))
                evacuated(pe, t, (a, "o", 3))
                for i in range(NT):
                    for k in range(CT):
                        last = pe.matmul(g[:, i * D:(i + 1) * D], oT[a][:, k, i * P:(i + 1) * P], wout[:, k, :],
                                         start=(k == 0), stop=(k == CT - 1))
                filled(last, u)

            for u in ahead_units:
                project(u, 0)
            for t, final in turns(pe):
                T = tallies(t)

                def scores(grp):
                    a, w = grp // 4, (grp % 4) // 2
                    units = [(a, "S", 4 * (grp % 4) + j) for j in range(4)]
                    gs = []
                    for x in range(2):
                        for j in range(4):
                            if not x:
                                gs.append(acquire(pe, t, units[j]))
                            c = 2 * (2 * (grp % 2) + j // 2) + x
                            r = slice(64 * (j % 2), 64 * (j % 2) + 64)
                            last = pe.matmul(gs[j][:, x * KEYS2:(x + 1) * KEYS2], qT[a][r, c, w * P:(w + 1) * P],
                                             kT[a][r, c, w, :], start=True, stop=True)
                            if x:
                                filled(last, units[j])

                def turn_probs(u):
                    a, i = divmod(u, 16)
                    g = acquire(pe, t, (a, "pt", i))[:].rearrange("p (x k s) -> p x k s", x=2, k=2)
                    evacuated(pe, t, (a, "S", i))
                    for x in range(2):
                        pe.transpose(g[0:PM, x, 1, :], probs[u % 8][:, x, 0:PM], ident[:])
                        last = pe.transpose(g[:, x, 0, :], probs[u % 8][:, x, PM:KEYS2], ident[:])
                    filled(last, (a, "pt", i))

                def pv(u):
                    a, i = divmod(u, 16)
                    grp = u // 4
                    if u % 4 == 0:
                        acquire(pe, t, (a, "o", i // 4))
                    if u >= 30:
                        evacuated(pe, t, (a, "pt", i))
                    w, j = (grp % 4) // 2, u % 4
                    for x in range(2):
                        hl = 4 * (j // 2) + 2 * x + j % 2
                        hd = 8 * (grp % 2) + hl
                        m = hl // 2
                        out = bank[6 + grp % 2][64 * (j % 2):64 * (j % 2) + 64, m * P:(m + 1) * P]
                        pe.matmul(out, v[a][:, w, hd * DH2:(hd + 1) * DH2], pts[u % 4][:, x, 0, :], start=True, stop=False)
                        last = pe.matmul(out, pmv[:, hd * DH2:(hd + 1) * DH2], pts[u % 4][0:PM, x, 1, :], start=False, stop=True)
                    if j == 3:
                        filled(last, (a, "o", i // 4))

                def r_T(grp):
                    u = (grp // 4, "rT", grp % 4)
                    g = acquire(pe, t, u)
                    T["rb_ready"].wait(pe, grp + 1)
                    for m in range(4):
                        last = pe.transpose(g[:, m * P:(m + 1) * P], rb[grp % 2][:, 2 * m:2 * m + 2, :], ident[:])
                    filled(last, u)

                def fill(units):
                    for *u, ahead in units:
                        if not (ahead and final):
                            project(tuple(u), t + ahead)

                for grp in range(9):
                    if grp < 8:
                        scores(grp)
                    for j in range(4):
                        if grp >= 1:
                            u = 4 * (grp - 1) + j
                            turn_probs(u)
                            if u >= 2:
                                pv(u - 2)
                        if grp >= 2 and j == 1:
                            r_T(grp - 2)
                        fill(between.get((grp, j), ()))
                r_T(7)
                pv(30)
                pv(31)
                fill(tail)
                project_out(1, t)

        @block.scalar
        def _(act):
            act.wait_ge(s_const, 16 * NCONST)

            def evacuate(u, t):
                a, n, i = u
                if n == "yT":
                    g = take(act, t, u)
                    for k in range(KD):
                        last = nc.scalar.activation(yT[a][:, k, :], g[:, k * S:(k + 1) * S], ACT.Copy, scale=gamma[:, k:k + 1])
                    release(last, u)
                if n == "q":
                    g = take(act, t, u)
                    release(nc.scalar.activation(qT[a][:, 2 * i:2 * i + 2, :], g[:].rearrange("p (x s) -> p x s", x=2),
                                                 ACT.Copy, scale=float(DH2 ** -0.5)), u)
                if n == "v" and i % 2 == 0:
                    g = take(act, t, u)
                    release(nc.scalar.activation(v[a][:, i // 2, 0:512], g[:], ACT.Copy), u)

            for u in ahead_units:
                evacuate(u, 0)
            for t, final in turns(act):
                T = tallies(t)

                def fill(units):
                    for *u, ahead in units:
                        if not (ahead and final):
                            evacuate(tuple(u), t + ahead)

                def exps(u):
                    a, i = divmod(u, 16)
                    un = (a, "S", i)
                    T["max_ready"].wait(act, u + 1)
                    g = bank[place[un][0]]
                    base = (i // 2) * 4 + i % 2
                    for x in range(2):
                        col = base + 2 * x
                        last = nc.scalar.activation(probs[u % 8][:, x, :], g[:, x * KEYS2:(x + 1) * KEYS2], ACT.Exp,
                                                    bias=nmax[a][:, col:col + 1], accum_out=rsum[a][:, col:col + 1])
                    release(last, un)

                def copy_pt(u):
                    un = (u // 16, "pt", u % 16)
                    g = take(act, t, un)[:].rearrange("p (x k s) -> p x k s", x=2, k=2)
                    nc.scalar.activation(pts[u % 4][0:PM, :, 1, :], g[0:PM, :, 1, :], ACT.Copy)
                    release(nc.scalar.activation(pts[u % 4][:, :, 0, :], g[:, :, 0, :], ACT.Copy), un)

                def r_out(grp):
                    u = (grp // 4, "rT", grp % 4)
                    g = take(act, t, u)
                    release(nc.scalar.activation(rT[grp % 2][:], g[:].rearrange("p (m s) -> p m s", m=4), ACT.Copy), u)

                for grp in range(9):
                    if grp < 8:
                        for j in range(4):
                            exps(4 * grp + j)
                            if grp >= 1 and j == 2:
                                copy_pt(4 * (grp - 1) + 1)
                    for j in range(4):
                        if grp >= 1 and (j == 3 or j == 1 and grp == 8):
                            copy_pt(4 * (grp - 1) + j)
                        if grp >= 2 and j == 1:
                            r_out(grp - 2)
                        fill(between.get((grp, j), ()))
                r_out(7)
                fill(tail)

        @block.vector
        def _(dve):
            for i in range(8):
                nc.vector.memset(scratch[:, i:i + 1], 0.0).then_inc(s_free[i], made_on["before", i][0] + 1)
                if made_on["before", i][0]:
                    nc.vector.memset(scratch[:, 9 + i:10 + i], 0.0).then_inc(s_full[i], made_on["before", i][0])
            dve.wait_ge(s_const, 16 * NCONST)
            for a in range(2):
                last = nc.vector.tensor_copy(kT[a][:, :, 0, 0:PM], pmk[:, :, 0, :])
                last = nc.vector.tensor_copy(kT[a][:, :, 1, 0:PM], pmk[:, :, 0, :])
            last.then_inc(sems["dve_step"], 1)

            def after_held(chain):
                chain.wait(dve)
                chain.up(nc.vector.memset(scratch[:, 8:9], 0.0))

            def stats_of(chain, a, s, mvs):
                after_held(chain)
                for i in range(NT):
                    last = nc.vector.bn_stats(stats[a][:, i, :], h[:, s, i, :])
                chain.up(last)
                after_held(chain)
                for i in range(NT):
                    last = nc.vector.bn_aggr(mvs[a][:, i, :], stats[a][:, i, :])
                return last

            def encoder_norm(chain, T, a, s):
                T["sd_ready"].wait(dve, 1 + 2 * a)
                chain.up(nc.vector.tensor_scalar(den[a][:], sd[a][:], float((D / (D - 1)) ** 0.5), TOK_EPS, ALU.mult, ALU.add))
                chain.wait(dve)
                chain.up(nc.vector.reciprocal(rstd[a][:], den[a][:]))
                chain.wait(dve)
                for i in range(NT):
                    last = nc.vector.tensor_scalar(h[:, s, i, :], h[:, s, i, :], mv[a][:, i, 0:1],
                                                   rstd[a][:, i:i + 1], ALU.subtract, ALU.mult)
                chain.up(last)

            def affine(chain, s):
                chain.wait(dve)
                chain.up(nc.vector.tensor_tensor(h[:, s], h[:, s], normab[:, 0:1, :].to_broadcast((P, NT, D)), ALU.mult))
                chain.wait(dve)
                chain.up(nc.vector.tensor_tensor(h[:, s], h[:, s], normab[:, 1:2, :].to_broadcast((P, NT, D)), ALU.add))

            def norms(chain, a, s):
                chain.up(stats_of(chain, a, s, mv2))
                chain.wait(dve)
                chain.up(nc.vector.tensor_scalar(den[a][:], mv2[a][:, :, 1], LN_EPS, RMS_EPS, ALU.add, ALU.mult))
                chain.wait(dve)
                nc.vector.tensor_tensor(den[a][:], den[a][:], mv2[a][:, :, 1], ALU.add).then_inc(sems["var_ready"], 1)

            def normalise(T, a, s):
                T["sd_ready"].wait(dve, 2 + 2 * a)
                for i in range(NT):
                    last = nc.vector.tensor_scalar(yn[a][:, i, :], h[:, s, i, :], mv2[a][:, i, 0:1],
                                                   sd2[a][:, i:i + 1], ALU.subtract, ALU.mult)
                last.then_inc(sems["yn_ready"], 1)

            def norm_step(chain, t, n, a):
                T = tallies(t)
                T["sd_ready"].credit = 2
                s = 2 * t + a
                if n == 0:
                    stats_of(chain, a, s, mv).then_inc(sems["var_ready"], 1)
                if n == 1:
                    encoder_norm(chain, T, a, s)
                if n == 2:
                    affine(chain, s)
                if n == 3:
                    norms(chain, a, s)
                if n == 4:
                    normalise(T, a, s)

            norm_at = {(0, 0): (0, 0), (0, 2): (1, 0), (0, 3): (2, 0), (1, 3): (3, 0), (2, 3): (4, 0),
                       (3, 1): (0, 1), (4, 3): (1, 1), (5, 1): (2, 1), (5, 3): (3, 1), (6, 3): (4, 1)}

            def evacuate(u, t):
                a, n, i = u
                if n == "k":
                    g = take(dve, t, u)
                    release(nc.vector.tensor_copy(kT[a][:, 2 * i:2 * i + 2, :, PM:],
                                                  g[:].rearrange("p (x w s) -> p x w s", x=2, w=2)), u)
                if n == "v" and i % 2:
                    g = take(dve, t, u)
                    release(nc.vector.tensor_copy(v[a][:, i // 2, 512:], g[:]), u)
                if n == "wo":
                    g = take(dve, t, u)
                    release(nc.vector.tensor_tensor(h[:, 2 * t + a], h[:, 2 * t + a], g[:].rearrange("p (i d) -> p i d", i=NT), ALU.add), u)

            start = Tally(sems["dve_step"], 0)
            start.n = 1
            for n, a in ((n, a) for a in range(2) for n in range(5)):
                norm_step(start, 0, n, a)
            assert start.n == FIRST, start.n
            for u in ahead_units:
                evacuate(u, 0)
            for t, final in turns(dve):
                T = tallies(t)
                chain = T["dve_step"]
                chain.credit = FIRST

                def link(ins):
                    chain.up(ins)

                def after():
                    chain.wait(dve)

                def fill(units):
                    for *u, ahead in units:
                        if not (ahead and final):
                            evacuate(tuple(u), t + ahead)

                def mask_scores(u):
                    a, i = divmod(u, 16)
                    g = take(dve, t, (a, "S", i))
                    gv = g[:, 0:2 * KEYS2].rearrange("p (x s) -> p x s", x=2)
                    link(nc.vector.tensor_tensor(gv, gv, mask[:].to_broadcast((P, 2, KEYS2)), ALU.add))

                def row_max(u):
                    a, i = divmod(u, 16)
                    after()
                    g = bank[place[(a, "S", i)][0]]
                    base = (i // 2) * 4 + i % 2
                    nc.vector.tensor_reduce(nmax[a][:, base:base + 3:2], g[:, 0:2 * KEYS2].rearrange("p (x s) -> p x s", x=2),
                                            AX.X, ALU.max, negate=True).then_inc(sems["max_ready"], 1)

                def copy_pt(u):
                    un = (u // 16, "pt", u % 16)
                    g = take(dve, t, un)[:].rearrange("p (x k s) -> p x k s", x=2, k=2)
                    nc.vector.tensor_copy(pts[u % 4][0:PM, :, 1, :], g[0:PM, :, 1, :])
                    release(nc.vector.tensor_copy(pts[u % 4][:, :, 0, :], g[:, :, 0, :]), un)

                def recips(grp):
                    a, i = grp // 4, grp % 4
                    evacuated(dve, t, (a, "S", 4 * i + 3))
                    link(nc.vector.reciprocal(rinv[a][:, 8 * i:8 * i + 8], rsum[a][:, 8 * i:8 * i + 8]))
                    after()
                    nc.vector.tensor_copy(rb[grp % 2][:], rinv[a][:, 8 * i:8 * i + 8].rearrange("p (n x) -> p n x", x=1)
                                          .to_broadcast((P, 8, DH2))).then_inc(sems["rb_ready"], 1)

                def o_norm(grp):
                    a, w, half = grp // 4, (grp % 4) // 2, grp % 2
                    evacuated(dve, t, (a, "rT", grp % 4))
                    g = take(dve, t, (a, "o", grp % 4))
                    release(nc.vector.tensor_tensor(oT[a][:, 4 * half:4 * half + 4, w * P:(w + 1) * P],
                                                    g[:].rearrange("p (m s) -> p m s", m=4), rT[grp % 2][:],
                                                    ALU.mult), (a, "o", grp % 4))

                for grp in range(9):
                    if grp < 8:
                        for j in range(4):
                            mask_scores(4 * grp + j)
                            row_max(4 * grp + j)
                            if grp >= 1 and j == 2:
                                copy_pt(4 * (grp - 1))
                    if grp >= 1:
                        recips(grp - 1)
                    for j in range(4):
                        if grp >= 1 and (j == 2 or j == 0 and grp == 8):
                            copy_pt(4 * (grp - 1) + j)
                        fill(between.get((grp, j), ()))
                        if (grp, j) in norm_at and not final:
                            norm_step(chain, t + 1, *norm_at[grp, j])
                    if grp >= 2:
                        o_norm(grp - 2)
                o_norm(7)
                fill(tail)
                evacuate((1, "wo", 0), t)
                if not final:
                    chain.whole()


class Ring:

    def __init__(self, banks, full, free, order):
        assert len(order) % len(banks) == 0
        self.banks, self.full, self.free = banks, full, free
        self.uses = len(order) // len(banks)
        self.place = {u: (i % len(banks), i // len(banks)) for i, u in enumerate(order)}

    def acquire(self, pe, t, u):
        b, use = self.place[u]
        pe.wait_ge(self.free[b], t * self.uses + use + 1)
        return self.banks[b]

    def filled(self, ins, u):
        ins.then_inc(self.full[self.place[u][0]], 1)

    def take(self, eng, t, u):
        b, use = self.place[u]
        eng.wait_ge(self.full[b], t * self.uses + use + 1)
        return self.banks[b]

    def release(self, ins, u):
        ins.then_inc(self.free[self.place[u][0]], 1)

    def evacuated(self, eng, t, u):
        b, use = self.place[u]
        eng.wait_ge(self.free[b], t * self.uses + use + 2)


class Chain:

    def __init__(self, eng, sem):
        self.eng, self.sem, self.n = eng, sem, 0

    def __call__(self, ins):
        ins.then_inc(self.sem, 1)
        self.n += 1
        self.eng.wait_ge(self.sem, self.n)


class ExpertLoads:

    def __init__(self, io, XS, sb, sem):
        self.io, self.XS = io, XS
        self.we = [sb(f"we{a}", [P, 6 * HID]) for a in range(2)]
        self.rows = [sb(f"xrows{a}", [P, -(-CAP // P), D]) for a in range(2)]
        self.s_up = [sem(f"e_up{a}") for a in range(2)]
        self.s_down = [sem(f"e_down{a}") for a in range(2)]
        self.s_rows = [sem(f"e_rows{a}") for a in range(2)]
        self.s_scat = sem("e_scat")

    def up(self, sp, e, a):
        sp.dma_start(self.we[a][:, 0:4 * HID], self.io["experts"][e, :, 0:4 * HID].rearrange("e p n -> p (e n)")).then_inc(self.s_up[a], 16)

    def down(self, sp, e, a):
        sp.dma_start(self.we[a][:, 4 * HID:], self.io["experts"][e, :, 4 * HID:].rearrange("e p n -> p (e n)")).then_inc(self.s_down[a], 16)

    def places(self, sp, e, a):
        full = CAP // P
        src = self.XS.rearrange("(e r) d -> e r d", e=E)[e]
        sp.dma_start(self.rows[a][:, 0:full, :], src[:, 0:full * P, :].rearrange("e (i p) d -> p (e i) d", p=P)).then_inc(self.s_rows[a], 16)
        sp.dma_start(self.rows[a][0:CAP - full * P, full, :], src[:, full * P:, :].rearrange("e r d -> (e r) d")).then_inc(self.s_rows[a], 16)


def mixture(nc, io, h):
    XS = nc.dram_tensor("expert_rows", [E * CAP, D], F32).ap()
    YS = nc.dram_tensor("expert_outs", [E * CAP + 1, D], F32).ap()
    T16 = B * NT
    with ExitStack() as ctx:
        sb = lambda name, shape, dt=F32: ctx.enter_context(nc.sbuf_tensor(name, shape, dt))
        x_all = sb("x_all", [P, T16, D])
        ident = sb("m_ident", [P, P])
        zeros = sb("zeros", [P, 4, D])
        wsel = [sb(f"wsel{k}", [P, T16]) for k in range(TOPK)]
        slot_u = [sb(f"slot_u{k}", [P, T16], U32) for k in range(TOPK)]
        s_zero = ctx.enter_context(nc.semaphore("m_zero"))
        loads = ExpertLoads(io, XS, sb, lambda name: ctx.enter_context(nc.semaphore(name)))
        with ExitStack() as c2:
            sb2 = lambda name, shape, dt=F32: c2.enter_context(nc.sbuf_tensor(name, shape, dt))
            xT = sb2("xT_all", [P, KD, N])
            shared = sb2("shared", [P, SHARED, 6 * HID])
            s_shared = c2.enter_context(nc.semaphore("m_shared"))
            keys = sb2("keys", [P, T16, E])
            pick = [sb2(f"pick{k}", [P, T16, E]) for k in range(TOPK)]
            gate(nc, io, h, x_all, xT, ident, zeros, XS, YS, s_zero, shared, s_shared, keys, pick, wsel)
            shared_and_slots(nc, io, h, x_all, xT, ident, XS, s_zero, shared, s_shared, keys, pick, slot_u, loads)
        experts(nc, io, h, ident, YS, wsel, slot_u, loads)


def gate(nc, io, h, x_all, xT, ident, zeros, XS, YS, s_zero, shared, s_shared, keys, pick, wsel):
    ctx = ExitStack()
    T16 = B * NT
    with ctx:
        sb = lambda name, shape, dt=F32: ctx.enter_context(nc.sbuf_tensor(name, shape, dt))
        sem = lambda name: ctx.enter_context(nc.semaphore(name))
        gw = sb("gw", [P, KD, E])
        gb = sb("gb", [P, 1, E])
        iota = sb("iota", [P, 1, E])
        expo = sb("g_expo", [P, NT])
        scratch = sb("g_scratch", [P, 8])
        xn = [sb(f"xn{a}", [P, NT, D]) for a in range(2)]
        xs = [sb(f"xs{a}", [P, KD, S]) for a in range(2)]
        stats = [sb(f"g_stats{a}", [P, NT, 6]) for a in range(2)]
        mv = [sb(f"g_mv{a}", [P, NT, 2]) for a in range(2)]
        ve = [sb(f"g_ve{a}", [P, NT]) for a in range(2)]
        rs = [sb(f"g_rs{a}", [P, NT]) for a in range(2)]
        logit = sb("logit", [P, T16, E])
        lmax = sb("lmax", [P, T16])
        lexp = sb("lexp", [P, T16, E])
        lsum = sb("lsum", [P, T16])
        score = sb("score", [P, T16, E])
        top = sb("top", [P, T16, 8])
        topi = sb("topi", [P, T16, 8], U32)
        topf = sb("topf", [P, T16, 8])
        work = sb("g_work", [P, T16, E])
        banks = [ctx.enter_context(nc.psum_tensor(f"g_bank{i}", [P, 512], F32)) for i in range(4)]
        ring = Ring(banks, [sem(f"g_full{i}") for i in range(4)], [sem(f"g_free{i}") for i in range(4)],
                    [(0, "xT"), (1, "xT"), (0, "lg"), (1, "lg")])
        s_const, s_var, s_sd, s_xn = sem("g_const"), sem("g_var"), sem("g_sd"), sem("g_xn")
        s_step, s_lexp, s_logits, s_lsub = sem("g_step"), sem("g_lexp"), sem("g_logits"), sem("g_lsub")
        PER = 8
        block = ctx.enter_context(nc.Block())

        @block.sync
        def _(sp):
            sp.dma_start(ident[:], io["ident"]).then_inc(s_const, 16)
            sp.dma_start(gw[:], io["gate_w"]).then_inc(s_const, 16)
            sp.dma_start(gb[:], io["gate_b"].partition_broadcast(P)).then_inc(s_const, 16)
            sp.dma_start(iota[:], io["iota"].partition_broadcast(P)).then_inc(s_const, 16)
            sp.dma_start(shared[:], io["shared"]).then_inc(s_shared, 16)
            sp.wait_ge(s_zero, 1)
            for r in range(0, E * CAP, 4 * P):
                sp.dma_start(XS[r:r + 4 * P, :].rearrange("(p r) d -> p r d", r=4), zeros[:]).then_inc(s_zero, 16)
            sp.dma_start(YS[E * CAP:, :], zeros[0:1, 0, :]).then_inc(s_zero, 16)

        @block.gpsimd
        def _(pool):
            nc.gpsimd.memset(zeros[:], 0.0).then_inc(s_zero, 1)
            nc.gpsimd.memset(expo[:], -0.5).then_inc(s_sd, 1)
            pool.wait_ge(s_sd, 1)
            with pool.Fori(0, PAIRS) as t:
                for a in range(2):
                    pool.wait_ge(s_var, 2 * t + a + 1)
                    nc.gpsimd.tensor_tensor(rs[a][:], ve[a][:], expo[:], ALU.pow).then_inc(s_sd, 1)

        @block.tensor
        def _(pe):
            pe.wait_ge(s_const, 64)
            with pe.Fori(0, PAIRS) as t:
                for a in range(2):
                    g = ring.acquire(pe, t, (a, "xT"))
                    pe.wait_ge(s_xn, 2 * t + a + 1)
                    for k in range(KD):
                        for i in range(NT):
                            last = pe.transpose(g[:, k * S + i * P:k * S + i * P + P], xn[a][:, i, k * P:(k + 1) * P], ident[:])
                    ring.filled(last, (a, "xT"))
                for a in range(2):
                    g = ring.acquire(pe, t, (a, "lg"))
                    ring.evacuated(pe, t, (a, "xT"))
                    for i in range(NT):
                        for k in range(KD):
                            last = pe.matmul(g[:, i * E:(i + 1) * E], xs[a][:, k, i * P:(i + 1) * P], gw[:, k, :],
                                             start=(k == 0), stop=(k == KD - 1))
                    ring.filled(last, (a, "lg"))

        @block.scalar
        def _(act):
            with act.Fori(0, PAIRS) as t:
                for a in range(2):
                    g = ring.take(act, t, (a, "xT"))
                    gv = g[:].rearrange("p (k s) -> p k s", k=KD)
                    nc.scalar.activation(xs[a][:], gv, ACT.Copy)
                    ring.release(nc.scalar.activation(xT[:, :, bass.ds((2 * t + a) * S, S)], gv, ACT.Copy), (a, "xT"))
                for a in range(2):
                    g = ring.take(act, t, (a, "lg"))
                    ring.release(nc.scalar.activation(logit[:, bass.ds((2 * t + a) * NT, NT), :],
                                                      g[:, 0:NT * E].rearrange("p (i e) -> p i e", i=NT), ACT.Copy), (a, "lg"))
            act.wait_ge(s_lsub, 1)
            nc.scalar.activation(lexp[:], work[:], ACT.Exp).then_inc(s_lexp, 1)

        @block.vector
        def _(dve):
            for i in range(4):
                nc.vector.memset(scratch[:, i:i + 1], 0.0).then_inc(ring.free[i], 1)
            nc.vector.memset(scratch[:, 6:7], 0.0).then_inc(s_step, 1)
            with dve.Fori(0, PAIRS) as t:
                n = 0

                def link(ins):
                    nonlocal n
                    ins.then_inc(s_step, 1)
                    n += 1

                def after():
                    dve.wait_ge(s_step, t * PER + n + 1)

                def after_held():
                    after()
                    link(nc.vector.memset(scratch[:, 6:7], 0.0))

                for a in range(2):
                    after_held()
                    for i in range(NT):
                        last = nc.vector.bn_stats(stats[a][:, i, :], h[:, 2 * t + a, i, :])
                    link(last)
                    after_held()
                    for i in range(NT):
                        last = nc.vector.bn_aggr(mv[a][:, i, :], stats[a][:, i, :])
                    link(last)
                    after()
                    nc.vector.tensor_scalar(ve[a][:], mv[a][:, :, 1], LN_EPS, None, ALU.add).then_inc(s_var, 1)
                for a in range(2):
                    dve.wait_ge(s_sd, 2 * t + a + 2)
                    for i in range(NT):
                        nc.vector.tensor_scalar(x_all[:, (2 * t + a) * NT + i, :], h[:, 2 * t + a, i, :], mv[a][:, i, 0:1],
                                                rs[a][:, i:i + 1], ALU.subtract, ALU.mult)
                    ring.acquire(dve, t, (a, "xT"))
                    for i in range(NT):
                        last = nc.vector.tensor_scalar(xn[a][:, i, :], h[:, 2 * t + a, i, :], mv[a][:, i, 0:1],
                                                       rs[a][:, i:i + 1], ALU.subtract, ALU.mult)
                    last.then_inc(s_xn, 1)
                assert n == PER, n
            for a in range(2):
                dve.wait_ge(ring.free[2 + a], PAIRS + 1)
            do = Chain(dve, s_logits)
            spread = lambda m: m[:].rearrange("p (t x) -> p t x", x=1).to_broadcast((P, T16, E))
            do(nc.vector.tensor_reduce(lmax[:], logit[:], AX.X, ALU.max))
            nc.vector.tensor_tensor(work[:], logit[:], spread(lmax), ALU.subtract).then_inc(s_lsub, 1)
            dve.wait_ge(s_const, 64)
            dve.wait_ge(s_lexp, 1)
            do(nc.vector.tensor_reduce(lsum[:], lexp[:], AX.X, ALU.add))
            do(nc.vector.reciprocal(lmax[:], lsum[:]))
            do(nc.vector.tensor_tensor(work[:], lexp[:], spread(lmax), ALU.mult))
            do(nc.vector.tensor_tensor(score[:], work[:], gb[:].to_broadcast((P, T16, E)), ALU.add))
            for i in range(T16):
                last = nc.vector.max(top[:, i, :], score[:, i, :])
            do(last)
            for i in range(T16):
                last = nc.vector.max_index(topi[:, i, :], top[:, i, :], score[:, i, :])
            do(last)
            do(nc.vector.tensor_copy(topf[:], topi[:]))
            for k in range(TOPK):
                do(nc.vector.tensor_tensor(pick[k][:], iota[:].to_broadcast((P, T16, E)),
                                           topf[:, :, k:k + 1].to_broadcast((P, T16, E)), ALU.is_equal))
                do(nc.vector.tensor_tensor(work[:], pick[k][:], logit[:], ALU.mult))
                do(nc.vector.tensor_reduce(wsel[k][:], work[:], AX.X, ALU.add))
            do(nc.vector.tensor_tensor(score[:], pick[0][:], pick[1][:], ALU.add))
            do(nc.vector.tensor_tensor(work[:], score[:], logit[:], ALU.mult))
            do(nc.vector.tensor_scalar(lexp[:], score[:], 1.0, -NEG, ALU.subtract, ALU.mult))
            do(nc.vector.tensor_tensor(keys[:], work[:], lexp[:], ALU.add))


def shared_and_slots(nc, io, h, x_all, xT, ident, XS, s_zero, shared, s_shared, keys, pick, slot_u, loads):
    ctx = ExitStack()
    T16 = B * NT
    STEPS = 32
    with ctx:
        sb = lambda name, shape, dt=F32: ctx.enter_context(nc.sbuf_tensor(name, shape, dt))
        sem = lambda name: ctx.enter_context(nc.semaphore(name))
        same = sb("same", [P, P])
        before = sb("before", [P, P])
        bits = sb("bits", [P, STEPS + 1], I32)
        base = sb("base", [P, 1])
        ones = sb("ones", [P, P])
        kT = sb("keysT", [P, 2, P])
        junk = sb("junk", [P, 2, P])
        found = sb("found", [P, 1], I32)
        trial = sb("trial", [P, 1], I32)
        passed = sb("passed", [P, 1], I32)
        cnt = sb("cnt", [P, 1])
        gt = sb("gt", [P, 2, P])
        eq = sb("eq", [P, 2, P])
        run = sb("run", [P, 2, P])
        tot = sb("tot", [P, 2])
        off = sb("off", [P, 2])
        need = sb("need", [P, 1])
        asg = sb("asg", [P, 2, P])
        keep = sb("keep", [P, 2, P])
        slots = sb("slots", [P, 2, P])
        slotm = sb("slotm", [P, T16, E])
        work = sb("s_work", [P, T16, E])
        slotf = sb("slotf", [P, T16])
        w1 = [shared[:, e, 0:KD * HID].rearrange("p (k n) -> p k n", k=KD) for e in range(SHARED)]
        w3 = [shared[:, e, KD * HID:2 * KD * HID].rearrange("p (k n) -> p k n", k=KD) for e in range(SHARED)]
        w2 = [shared[:, e, 2 * KD * HID:].rearrange("p (k n) -> p k n", k=HT) for e in range(SHARED)]
        silu = [sb(f"silu{i}", [P, S]) for i in range(4)]
        gT = [sb(f"gT{a}", [P, SHARED * HT, S]) for a in range(2)]
        scratch = sb("s_scratch", [P, 8])
        NB = 6
        banks = [ctx.enter_context(nc.psum_tensor(f"s_bank{i}", [P, 512], F32)) for i in range(NB)]
        sps = ctx.enter_context(nc.psum_tensor("sps", [P, 512], F32))
        UP = SHARED * HT
        order = [(a, "up", i) for a in (0, 1) for i in range(UP)] + [(0, "down", 0), (1, "down", 0)]
        ring = Ring(banks, [sem(f"s_full{i}") for i in range(NB)], [sem(f"s_free{i}") for i in range(NB)], order)
        s_const, s_keysT, s_cnt, s_tot, s_step, s_silu = (sem(n) for n in
            ("s_const2", "s_keysT", "s_cnt", "s_tot", "s_step2", "s_silu"))
        s_tail, s_off, s_slots = sem("s_tail"), sem("s_off"), sem("s_slots")
        SEARCH = 2
        PER_TURN = STEPS // SEARCH
        step_at = {n: i for i, n in enumerate([n for n in range(2 * UP) if n % 4 != 3] + list(range(2 * UP, 2 * UP + 2 * NT)))}
        assert len(step_at) == PER_TURN
        block = ctx.enter_context(nc.Block())

        @block.sync
        def _(sp):
            for dst, src in ((same, "same"), (before, "before"), (bits, "bits"), (base, "base")):
                sp.dma_start(dst[:], io[src]).then_inc(s_const, 16)
            for a in range(2):
                loads.up(sp, slice(a, a + 1), a)
                loads.down(sp, slice(a, a + 1), a)
            sp.wait_ge(loads.s_scat, 16 * TOPK * T16)
            for a in range(2):
                loads.places(sp, slice(a, a + 1), a)

        @block.gpsimd
        def _(pool):
            pool.wait_ge(s_zero, 1 + 16 * (E * CAP // (4 * P) + 1))
            pool.wait_ge(s_slots, 1)
            for j in range(T16):
                for k in range(TOPK):
                    pool.indirect_dma_start(XS, bass.IndirectOffsetOnAxis(ap=slot_u[k][:, j:j + 1], axis=0), x_all[:, j, :], None,
                                            bounds_check=E * CAP - 1, oob_is_err=False).then_inc(loads.s_scat, 16)

        @block.tensor
        def _(pe):
            kv = keys[:].rearrange("p (x t) e -> p x (t e)", x=2)
            for x in range(2):
                last = pe.transpose(sps[:, x * P:(x + 1) * P], kv[:, x, :], ident[:])
            last.then_inc(s_keysT, 1)
            pe.wait_ge(s_const, 64)
            pe.wait_ge(s_shared, 16)

            def turn(t, between):
                for a in range(2):
                    for i in range(UP):
                        u = (a, "up", i)
                        e, m = divmod(i, HT)
                        g = ring.acquire(pe, t, u)
                        for x, w in ((0, w1), (1, w3)):
                            for k in range(KD):
                                last = pe.matmul(g[:, x * S:(x + 1) * S], w[e][:, k, m * P:(m + 1) * P],
                                                 xT[:, k, bass.ds((2 * t + a) * S, S)],
                                                 start=(k == 0), stop=(k == KD - 1))
                        ring.filled(last, u)
                        between(a * UP + i)
                for a in range(2):
                    u = (a, "down", 0)
                    g = ring.acquire(pe, t, u)
                    ring.evacuated(pe, t, (a, "up", UP - 1))
                    for i in range(NT):
                        for k in range(UP):
                            e, m = divmod(k, HT)
                            last = pe.matmul(g[:, i * D:(i + 1) * D], gT[a][:, k, i * P:(i + 1) * P], w2[e][:, m, :],
                                             start=(k == 0), stop=(k == UP - 1))
                        if i == NT - 1:
                            ring.filled(last, u)
                        between(2 * UP + a * NT + i)

            with pe.Fori(0, SEARCH) as t:
                def search(n):
                    if n in step_at:
                        pe.wait_ge(s_cnt, t * PER_TURN + step_at[n] + 1)
                        pe.matmul(sps[:, 0:1], same[:], cnt[:], start=True, stop=True).then_inc(s_tot, 1)
                turn(t, search)

            def sums(n):
                if n == 2:
                    pe.wait_ge(s_tail, 1)
                    pe.matmul(sps[:, 0:1], same[:], cnt[:], start=True, stop=True).then_inc(s_off, 1)
                if n in (6, 10):
                    pe.wait_ge(s_tail, 2 if n == 6 else 3)
                    pe.matmul(sps[:, 0:2], before[:], tot[:], start=True, stop=True)
                    pe.matmul(sps[:, 2:3], same[:], tot[:, 0:1], start=True, stop=True).then_inc(s_off, 1)
                if n == 13:
                    pe.wait_ge(s_tail, 4)
                    for x in range(2):
                        last = pe.transpose(sps[:, x * P:(x + 1) * P], slots[:, x, :], ident[:])
                    last.then_inc(s_off, 1)

            turn(SEARCH, sums)
            for t in range(SEARCH + 1, PAIRS):
                turn(t, lambda n: None)

        @block.scalar
        def _(act):
            with act.Fori(0, PAIRS) as t:
                for a in range(2):
                    for i in range(UP):
                        n = a * UP + i
                        g = ring.take(act, t, (a, "up", i))
                        if n >= 4:
                            prev = (n - 4) // UP, "up", (n - 4) % UP
                            ring.evacuated(act, t, prev)
                        nc.scalar.activation(silu[n % 4][:], g[:, 0:S], ACT.Silu).then_inc(s_silu, 1)

        @block.vector
        def _(dve):
            for i in range(NB):
                nc.vector.memset(scratch[:, i:i + 1], 0.0).then_inc(ring.free[i], 1)
            do = Chain(dve, s_step)
            nc.vector.memset(ones[:], 1.0)
            dve.wait_ge(s_const, 64)
            do(nc.vector.memset(found[:], -1))
            dve.wait_ge(s_keysT, 1)
            do(nc.vector.tensor_copy(kT[:], sps[:, 0:2 * P].rearrange("p (x s) -> p x s", x=2)))

            def count():
                nc.vector.tensor_scalar(junk[:], kT[:], trial[:].bitcast(F32), None, ALU.is_ge, ALU.add, accum_out=cnt[:]).then_inc(s_cnt, 1)

            do(nc.vector.tensor_tensor(trial[:], found[:], bits[:, 0:1], ALU.bitwise_xor))
            count()
            FIRST = do.n
            LINKS = 3

            def turn(t, between):
                for a in range(2):
                    for i in range(UP):
                        u = (a, "up", i)
                        dve.wait_ge(s_silu, t * (2 * UP) + a * UP + i + 1)
                        g = ring.banks[ring.place[u][0]]
                        ring.release(nc.vector.tensor_tensor(gT[a][:, i, :], g[:, S:2 * S], silu[(a * UP + i) % 4][:], ALU.mult), u)
                        between(a * UP + i)
                for a in range(2):
                    for i in range(NT):
                        between(2 * UP + a * NT + i)
                    u = (a, "down", 0)
                    g = ring.take(dve, t, u)
                    ring.release(nc.vector.scalar_tensor_tensor(out=h[:, 2 * t + a], in0=g[:].rearrange("p (i d) -> p i d", i=NT),
                                                                scalar=1.0 / SHARED, in1=h[:, 2 * t + a], op0=ALU.mult, op1=ALU.add), u)

            with dve.Fori(0, SEARCH) as t:
                def search(n):
                    if n not in step_at:
                        return
                    at = t * PER_TURN + step_at[n]
                    links = FIRST + at * LINKS
                    dve.wait_ge(s_tot, at + 1)
                    nc.vector.tensor_scalar(passed[:], sps[:, 0:1], float(CAP) - 0.5, -1.0, ALU.is_gt, ALU.mult).then_inc(s_step, 1)
                    dve.wait_ge(s_step, links + 1)
                    nc.vector.scalar_tensor_tensor(out=found[:], in0=bits[:, bass.ds(at, 1)], scalar=passed[:],
                                                   in1=found[:], op0=ALU.bitwise_and, op1=ALU.bitwise_xor).then_inc(s_step, 1)
                    dve.wait_ge(s_step, links + 2)
                    nc.vector.tensor_tensor(trial[:], found[:], bits[:, bass.ds(at + 1, 1)], ALU.bitwise_xor).then_inc(s_step, 1)
                    dve.wait_ge(s_step, links + 3)
                    count()
                turn(t, search)
            do.n = FIRST + STEPS * LINKS

            def ranked(src):
                for x in range(2):
                    last = nc.vector.tensor_tensor_scan(run[:, x, :], ones[:], src[:, x, :], 0.0, ALU.mult, ALU.add)
                do(last)
                nc.vector.tensor_copy(tot[:], run[:, :, P - 1]).then_inc(s_tail, 1)

            def offsets(n):
                dve.wait_ge(s_off, n)
                do(nc.vector.tensor_copy(off[:, 0:2], sps[:, 0:2]))
                do(nc.vector.tensor_tensor(off[:, 1:2], off[:, 1:2], sps[:, 2:3], ALU.add))

            def slot_step(n):
                if n == 0:
                    dve.wait_ge(s_step, do.n)
                    dve.wait_ge(s_cnt, STEPS + 1)
                    nc.vector.tensor_scalar(gt[:], kT[:], found[:].bitcast(F32), None, ALU.is_gt, ALU.add, accum_out=cnt[:]).then_inc(s_tail, 1)
                    do(nc.vector.tensor_scalar(eq[:], kT[:], found[:].bitcast(F32), None, ALU.is_equal))
                    do(nc.vector.tensor_scalar(asg[:], kT[:], NEG, None, ALU.is_gt))
                if n == 3:
                    dve.wait_ge(s_off, 1)
                    do(nc.vector.tensor_scalar(need[:], sps[:, 0:1], -1.0, float(CAP), ALU.mult, ALU.add))
                    ranked(eq)
                if n == 7:
                    offsets(2)
                    for x in range(2):
                        last = nc.vector.tensor_scalar(run[:, x, :], run[:, x, :], off[:, x:x + 1], need[:, 0:1], ALU.add, ALU.is_le)
                    do(last)
                    do(nc.vector.tensor_tensor(eq[:], eq[:], run[:], ALU.mult))
                    do(nc.vector.tensor_tensor(keep[:], gt[:], eq[:], ALU.add))
                    do(nc.vector.tensor_tensor(keep[:], keep[:], asg[:], ALU.mult))
                    ranked(keep)
                if n == 11:
                    offsets(3)
                    for x in range(2):
                        last = nc.vector.tensor_scalar(run[:, x, :], run[:, x, :], off[:, x:x + 1], base[:, 0:1], ALU.add, ALU.add)
                    do(last)
                    do(nc.vector.tensor_tensor(run[:], run[:], keep[:], ALU.mult))
                    nc.vector.tensor_scalar(slots[:], run[:], float(E * CAP), None, ALU.add).then_inc(s_tail, 1)
                if n == 14:
                    dve.wait_ge(s_off, 4)
                    do(nc.vector.tensor_copy(slotm[:], sps[:, 0:2 * P].rearrange("p (t e) -> p t e", e=E)))
                    for k in range(TOPK):
                        do(nc.vector.tensor_tensor(work[:], slotm[:], pick[k][:], ALU.mult))
                        do(nc.vector.tensor_reduce(slotf[:], work[:], AX.X, ALU.add))
                        ins = nc.vector.tensor_copy(slot_u[k][:], slotf[:])
                        if k < TOPK - 1:
                            do(ins)
                    ins.then_inc(s_slots, 1)

            turn(SEARCH, slot_step)
            for t in range(SEARCH + 1, PAIRS):
                turn(t, lambda n: None)


def experts(nc, io, h, ident, YS, wsel, slot_u, loads):
    ctx = ExitStack()
    T16 = B * NT
    RT = -(-CAP // P)
    ROWS = [min(P, CAP - i * P) for i in range(RT)]
    FULL = CAP // P
    with ctx:
        sb = lambda name, shape, dt=F32: ctx.enter_context(nc.sbuf_tensor(name, shape, dt))
        sem = lambda name: ctx.enter_context(nc.semaphore(name))
        we, rows, s_rows = loads.we, loads.rows, loads.s_rows
        w1 = [w[:, 0:KD * HID].rearrange("p (k n) -> p k n", k=KD) for w in we]
        w3 = [w[:, KD * HID:2 * KD * HID].rearrange("p (k n) -> p k n", k=KD) for w in we]
        w2 = [w[:, 2 * KD * HID:].rearrange("p (k n) -> p k n", k=HT) for w in we]
        xeT = [sb(f"xeT{a}", [P, KD, CAP]) for a in range(2)]
        silu = [sb(f"e_silu{i}", [P, CAP]) for i in range(4)]
        gT = [sb(f"e_gT{a}", [P, HT, CAP]) for a in range(2)]
        ye = [sb(f"ye{a}", [P, RT, D]) for a in range(2)]
        back = [sb(f"back{k}", [P, T16, D]) for k in range(TOPK)]
        scratch = sb("e_scratch", [P, 9])
        NB = 8
        banks = [ctx.enter_context(nc.psum_tensor(f"e_bank{i}", [P, 512], F32)) for i in range(NB)]
        order = [(a, "xT", k) for a in (0, 1) for k in range(KD)]
        order += [(a, "up", i) for a in (0, 1) for i in range(2 * HT)]
        order += [(a, "down", i) for a in (0, 1) for i in range(2)]
        ring = Ring(banks, [sem(f"e_full{i}") for i in range(NB)], [sem(f"e_free{i}") for i in range(NB)], order)
        s_stored, s_acc, s_out = (sem("e_" + n) for n in ("stored", "acc", "out"))
        TURNS = E // 2
        s_back = [sem(f"e_back{s}") for s in range(B)]
        block = ctx.enter_context(nc.Block())

        @block.sync
        def _(sp):
            with sp.Fori(0, TURNS - 1) as t:
                nxt = [bass.ds(2 * t + 2 + a, 1) for a in range(2)]
                for a in range(2):
                    ring.take(sp, t, (a, "xT", 1))
                    loads.places(sp, nxt[a], a)
                for a in range(2):
                    ring.take(sp, t, (a, "up", 2 * HT - 1))
                    loads.up(sp, nxt[a], a)
                for a in range(2):
                    ring.take(sp, t, (a, "down", 1))
                    loads.down(sp, nxt[a], a)

        @block.gpsimd
        def _(pool):
            pool.wait_ge(s_stored, 1 + 2 * 16 * E)
            for j in range(T16):
                for k in range(TOPK):
                    pool.indirect_dma_start(back[k][:, j, :], None, YS,
                                            bass.IndirectOffsetOnAxis(ap=slot_u[k][:, j:j + 1], axis=0)).then_inc(s_back[j // NT], 16)

        @block.tensor
        def _(pe):
            def rows_T(t, a):
                pe.wait_ge(s_rows[a], t * 32 + 32)
                for k in range(KD):
                    u = (a, "xT", k)
                    g = ring.acquire(pe, t, u)
                    for i in range(RT):
                        last = pe.transpose(g[:, i * P:i * P + ROWS[i]], rows[a][0:ROWS[i], i, k * P:(k + 1) * P],
                                            ident[0:ROWS[i], 0:ROWS[i]])
                    ring.filled(last, u)

            def turn(t, last_turn):
                for a in range(2):
                    pe.wait_ge(loads.s_up[a], t * 16 + 16)
                    for k in range(KD):
                        ring.evacuated(pe, t, (a, "xT", k))
                    for i in range(2 * HT):
                        m, x = divmod(i, 2)
                        u = (a, "up", i)
                        g = ring.acquire(pe, t, u)
                        for k in range(KD):
                            last = pe.matmul(g[:, 0:CAP], (w1, w3)[x][a][:, k, m * P:(m + 1) * P], xeT[a][:, k, :],
                                             start=(k == 0), stop=(k == KD - 1))
                        ring.filled(last, u)
                if not last_turn:
                    for a in range(2):
                        rows_T(t + 1, a)
                for a in range(2):
                    pe.wait_ge(loads.s_down[a], t * 16 + 16)
                    ring.evacuated(pe, t, (a, "up", 2 * HT - 1))
                    for half in range(2):
                        u = (a, "down", half)
                        g = ring.acquire(pe, t, u)
                        for i in ((0, 1) if half == 0 else (2,)):
                            for k in range(HT):
                                last = pe.matmul(g[0:ROWS[i], (i % 2) * D:(i % 2 + 1) * D], gT[a][:, k, i * P:i * P + ROWS[i]],
                                                 w2[a][:, k, :], start=(k == 0), stop=(k == HT - 1))
                        ring.filled(last, u)

            for a in range(2):
                rows_T(0, a)
            with pe.Fori(0, TURNS - 1) as t:
                turn(t, False)
            turn(TURNS - 1, True)

        @block.scalar
        def _(act):
            def rows_out(t):
                for a in range(2):
                    u = (a, "xT", 0)
                    g = ring.take(act, t, u)
                    ring.release(nc.scalar.activation(xeT[a][:, 0, :], g[:, 0:CAP], ACT.Copy), u)

            def turn(t, last_turn):
                for a in range(2):
                    for m in range(HT):
                        n = a * HT + m
                        u = (a, "up", 2 * m)
                        g = ring.take(act, t, u)
                        if n >= 4:
                            ring.evacuated(act, t, ((n - 4) // HT, "up", 2 * ((n - 4) % HT) + 1))
                        ring.release(nc.scalar.activation(silu[n % 4][:], g[:, 0:CAP], ACT.Silu), u)
                if not last_turn:
                    rows_out(t + 1)
                for a in range(2):
                    e = 2 * t + a
                    dst = YS[0:E * CAP, :].rearrange("(e r) d -> e r d", e=E)[bass.ds(e, 1)]
                    ring.evacuated(act, t, (a, "down", 1))
                    act.dma_start(dst[:, 0:FULL * P, :].rearrange("e (i p) d -> p (e i) d", p=P), ye[a][:, 0:FULL, :]).then_inc(s_stored, 16)
                    act.dma_start(dst[:, FULL * P:, :].rearrange("e r d -> (e r) d"), ye[a][0:ROWS[-1], FULL, :]).then_inc(s_stored, 16)

            rows_out(0)
            with act.Fori(0, TURNS - 1) as t:
                turn(t, False)
            turn(TURNS - 1, True)
            for s in range(B):
                act.wait_ge(s_acc, 2 * s + 2)
                act.dma_start(io["out"].rearrange("(s i p) d -> s p i d", p=P, i=NT)[s], h[:, s]).then_inc(s_out, 16)
            act.wait_ge(s_out, 16 * B)

        @block.vector
        def _(dve):
            for i in range(NB):
                nc.vector.memset(scratch[:, i:i + 1], 0.0).then_inc(ring.free[i], 1)
            nc.vector.memset(scratch[:, NB:NB + 1], 0.0).then_inc(s_stored, 1)

            def rows_out(t):
                for a in range(2):
                    u = (a, "xT", 1)
                    g = ring.take(dve, t, u)
                    ring.release(nc.vector.tensor_copy(xeT[a][:, 1, :], g[:, 0:CAP]), u)

            def turn(t, last_turn):
                for a in range(2):
                    for m in range(HT):
                        u = (a, "up", 2 * m + 1)
                        ring.evacuated(dve, t, (a, "up", 2 * m))
                        g = ring.take(dve, t, u)
                        ring.release(nc.vector.tensor_tensor(gT[a][:, m, :], g[:, 0:CAP], silu[(a * HT + m) % 4][:], ALU.mult), u)
                if not last_turn:
                    rows_out(t + 1)
                for a in range(2):
                    u = (a, "down", 0)
                    g = ring.take(dve, t, u)
                    dve.wait_ge(s_stored, t * 64 + 1)
                    ring.release(nc.vector.tensor_copy(ye[a][:, 0:FULL, :], g[:].rearrange("p (i d) -> p i d", i=2)), u)
                    u = (a, "down", 1)
                    g = ring.take(dve, t, u)
                    ring.release(nc.vector.tensor_copy(ye[a][0:ROWS[-1], FULL, :], g[0:ROWS[-1], 0:D]), u)

            rows_out(0)
            with dve.Fori(0, TURNS - 1) as t:
                turn(t, False)
            turn(TURNS - 1, True)
            for s in range(B):
                dve.wait_ge(s_back[s], 16 * NT * TOPK)
                for k in range(TOPK):
                    if k:
                        dve.wait_ge(s_acc, 2 * s + 1)
                    for i in range(NT):
                        j = s * NT + i
                        last = nc.vector.scalar_tensor_tensor(out=h[:, s, i, :], in0=back[k][:, j, :], scalar=wsel[k][:, j:j + 1],
                                                              in1=h[:, s, i, :], op0=ALU.mult, op1=ALU.add)
                    last.then_inc(s_acc, 1)


def build(nc, io):
    with ExitStack() as ctx:
        sb = lambda name, shape: ctx.enter_context(nc.sbuf_tensor(name, shape, F32))
        h = sb("h", [P, B, NT, D])
        with ExitStack() as c2:
            wqkv = c2.enter_context(nc.sbuf_tensor("wqkv", [P, KD, 3 * INNER], F32))
            wout = c2.enter_context(nc.sbuf_tensor("wout", [P, CT, D], F32))
            s_w2 = c2.enter_context(nc.semaphore("s_w2"))
            embed_and_encoder(nc, io, h, wqkv, wout, s_w2)
            windowed_attention(nc, io, h, wqkv, wout, s_w2)
        mixture(nc, io, h)


def layout(x):
    g = {k: np.asarray(a) for k, a in x.items()}
    cut = lambda w: w.reshape(*w.shape[:-2], w.shape[-2] // P, P, w.shape[-1]).swapaxes(-3, -2)
    t = {}
    t["idx"] = g["x"].reshape(B, NT, P).transpose(2, 0, 1).reshape(P, B * NT)
    t["emb"] = g["L0_tok_emb"]
    aw, w1, w2 = cut(g["L0_tok_attn_w"]), cut(g["L0_tok_w1"]), cut(g["L0_tok_w2"])
    t["wtok"] = np.concatenate([aw.transpose(0, 2, 1, 3, 4).reshape(L, P, -1),
                                w1.reshape(L, P, -1), w2.reshape(L, P, -1)], axis=2)
    col = lambda w: w.reshape(L, -1, P).transpose(0, 2, 1)
    ab = g["L0_tok_attn_b"]
    t["cols"] = np.concatenate([col(g["L0_tok_ln_a"]), col(g["L0_tok_ln_b"]), col(ab[:, 0]), col(ab[:, 1]),
                                col(g["L0_tok_b1"])], axis=2)
    t["rows"] = np.stack([ab[:, 2], ab[:, 3], g["L0_tok_b2"]], axis=1)
    pos = np.arange(S, dtype=np.float32)[:, None]
    div = np.exp(np.arange(0, D, 2, dtype=np.float32) * -(np.log(10000.0) / D))
    pe = np.zeros((S, D), np.float32)
    pe[:, 0::2], pe[:, 1::2] = np.sin(pos * div), np.cos(pos * div)
    t["pe"] = pe.reshape(NT, P, D).transpose(1, 0, 2)
    t["ident"] = np.eye(P, dtype=np.float32)
    t["qmask"] = ((np.arange(P) // DK)[:, None] % STRIP == np.arange(STRIP)).astype(np.float32) * np.float32(DK ** -0.5)
    t["wqkv"], t["wout"] = cut(g["L0_attn_w_qkv"]), cut(g["L0_attn_w_out"])
    t["gamma"] = g["L0_attn_gamma"].reshape(KD, P).T
    t["normab"] = np.stack([g["L0_tok_norm_a"], g["L0_tok_norm_b"]])
    t["pmk"] = g["L0_attn_pm_k"].reshape(CT, 2, PM, DH2).transpose(1, 3, 0, 2).reshape(P, CT, 1, PM)
    t["pmv"] = g["L0_attn_pm_v"].transpose(1, 0, 2).reshape(PM, INNER)
    ex = lambda p: [cut(g[f"L0_ffn_{p}w{i}"]) for i in (1, 3, 2)]
    t["experts"] = np.concatenate([w.reshape(E, P, -1) for w in ex("e")], axis=2)
    t["shared"] = np.concatenate([w.reshape(SHARED, P, -1) for w in ex("s")], axis=2).transpose(1, 0, 2)
    t["gate_w"], t["gate_b"] = cut(g["L0_ffn_gate_w"]), g["L0_ffn_gate_b"].reshape(1, E)
    t["iota"] = np.arange(E, dtype=np.float32).reshape(1, E)
    e, t8 = np.arange(P) % E, np.arange(P) // E
    same = e[:, None] == e[None, :]
    t["same"] = same.astype(np.float32)
    t["before"] = (same & (t8[:, None] < t8[None, :])).astype(np.float32)
    t["bits"] = np.broadcast_to(np.array([-1] + [1 << (31 - i) for i in range(1, 32)] + [0], np.int32), (P, 33))
    t["base"] = (e * CAP - 1 - E * CAP).astype(np.float32).reshape(P, 1)
    kj = np.arange(KEYS2)[None, :] - PM
    t["mask"] = np.where((kj < 0) | (np.arange(P)[:, None] >= kj), 0.0, NEG).astype(np.float32).reshape(P, 1, KEYS2)
    return {k: np.ascontiguousarray(a) for k, a in t.items()}


OUT = ((B * S, D), "float32")


def declare(nc, arrays):
    io = {k: nc.dram_tensor(f"in_{k}", a.shape, mybir.dt.from_np(a.dtype), kind="ExternalInput").ap()
          for k, a in arrays.items()}
    io["out"] = nc.dram_tensor("out_0", OUT[0], F32, kind="ExternalOutput").ap()
    return io


def kernel(**inputs):
    import concourse.bacc as bacc
    from concourse.bass_utils import run_bass_kernel_spmd as run
    nc = bacc.Bacc("TRN2", target_bir_lowering=False, num_devices=1)
    arrays = layout(inputs)
    build(nc, declare(nc, arrays))
    r = run(nc, [{f"in_{k}": a for k, a in arrays.items()}], core_ids=[0])
    return r.results[0]["out_0"].reshape(B, S, D)
```
